# Optimizing a Trainium2 kernel written in Bass

```python
import numpy as np
import jax
import jax.numpy as jnp

def _softmax(x, axis=-1):
    return jax.nn.softmax(x, axis=axis)

def _gelu(x):
    return jax.nn.gelu(x, approximate=True)

def _silu(x):
    return jax.nn.silu(x)

def _sigmoid(x):
    return jax.nn.sigmoid(x)

def _layernorm(x, axis=-1, eps=1e-05):
    m = jnp.mean(x, axis=axis, keepdims=True)
    v = jnp.var(x, axis=axis, keepdims=True)
    return (x - m) / jnp.sqrt(v + eps)

def _scatter_add(tgt, idx, src, axis=0):
    return tgt.at[idx].add(src)

def _segment_sum(src, seg, n):
    return jax.ops.segment_sum(src, seg, n)
kernel_name = 'mk_adj_preln_d2_adj_r2_470faf'

def setup_inputs(seed: int=0):
    np.random.seed(seed)
    _w = jnp.asarray

    def _rec_inputs():
        import jax
        import jax.numpy as jnp
        _gk = jax.random.key(seed)
        x = 7.22e-05 + 1 * jax.random.normal(jax.random.fold_in(_gk, 1), (16, 512, 256), jnp.float32)
        _a = jax.random.bernoulli(jax.random.fold_in(_gk, 2), 0.015625, (512, 512))
        adj = _a.astype(jnp.int32)
        return (x, adj)
    x, adj = _rec_inputs()

    def _L0_gnn_setup():
        import jax, jax.numpy as jnp
        import numpy as np
        LEAKY_ALPHA = 0.01
        NEG_INF = -1000000000.0
        LN_EPS = 1e-05

        def _gat_heads(x, adj, W, a):
            O = W.shape[-1]
            Wh = jnp.einsum('bnf,hfo->bhno', x, W)
            f1 = jnp.einsum('bhno,ho->bhn', Wh, a[:, :O])
            f2 = jnp.einsum('bhno,ho->bhn', Wh, a[:, O:])
            e = f1[:, :, :, None] + f2[:, :, None, :]
            e = jnp.where(e > 0, e, LEAKY_ALPHA * e)
            e = jnp.where(adj[None, None] > 0, e, NEG_INF)
            attn = jax.nn.softmax(e, axis=-1)
            return jnp.einsum('bhnm,bhmo->bhno', attn, Wh)
        key = jax.random.key(seed)
        ks = jax.random.split(key, 10)
        B, N, F_in, F_hid, H, F_out, D_ff = (8, 1024, 256, 256, 4, 256, 256)
        s = 0.05
        return {'enc_inputs': jax.random.normal(ks[0], (B, N, F_in), jnp.float32), 'adj': jax.random.randint(ks[1], (N, N), 0, 2, jnp.int32), 'W_heads': jax.random.normal(ks[2], (H, F_in, F_hid), jnp.float32) * s, 'a_heads': jax.random.normal(ks[3], (H, 2 * F_hid), jnp.float32) * s, 'W_out': jax.random.normal(ks[4], (H * F_hid, F_out), jnp.float32) * s, 'a_out': jax.random.normal(ks[5], (2 * F_out,), jnp.float32) * s, 'w1': jax.random.normal(ks[6], (F_out, D_ff), jnp.float32) * s, 'b1': jnp.zeros((D_ff,), jnp.float32), 'w2': jax.random.normal(ks[7], (D_ff, F_out), jnp.float32) * s, 'b2': jnp.zeros((F_out,), jnp.float32), 'ln_gamma': jnp.ones((F_out,), jnp.float32), 'ln_beta': jnp.zeros((F_out,), jnp.float32)}
    _L0_gnn_all = _L0_gnn_setup()
    _L0_gnn_in = {k: v for k, v in _L0_gnn_all.items() if k in ('W_heads', 'a_heads', 'W_out', 'a_out', 'w1', 'b1', 'w2', 'b2', 'ln_gamma', 'ln_beta')}
    del _L0_gnn_all

    def _L1_gnn_setup():
        import jax, jax.numpy as jnp
        import numpy as np
        B, K, DIN, DOUT = (32, 64, 256, 256)
        key = jax.random.key(seed)
        k1, k2, k3, k4 = jax.random.split(key, 4)
        x = jax.random.normal(k1, (B, K, DIN), dtype=jnp.float32)
        adj = jax.random.randint(k2, (K, K), 0, 2, dtype=jnp.int32)
        W = jax.random.normal(k3, (DOUT, 2 * DIN), dtype=jnp.float32) * 0.02
        b = jax.random.normal(k4, (DOUT,), dtype=jnp.float32) * 0.02
        return {'x': x, 'adj': adj, 'W': W, 'b': b}
    _L1_gnn_all = _L1_gnn_setup()
    _L1_gnn_in = {k: v for k, v in _L1_gnn_all.items() if k in ('W', 'b')}
    del _L1_gnn_all
    return {'x': x, 'adj': adj, 'L0_gnn_W_heads': _L0_gnn_in['W_heads'], 'L0_gnn_a_heads': _L0_gnn_in['a_heads'], 'L0_gnn_W_out': _L0_gnn_in['W_out'], 'L0_gnn_a_out': _L0_gnn_in['a_out'], 'L0_gnn_w1': _L0_gnn_in['w1'], 'L0_gnn_b1': _L0_gnn_in['b1'], 'L0_gnn_w2': _L0_gnn_in['w2'], 'L0_gnn_b2': _L0_gnn_in['b2'], 'L0_gnn_ln_gamma': _L0_gnn_in['ln_gamma'], 'L0_gnn_ln_beta': _L0_gnn_in['ln_beta'], 'L1_gnn_W': _L1_gnn_in['W'], 'L1_gnn_b': _L1_gnn_in['b']}

def reference(x, adj, L0_gnn_W_heads, L0_gnn_a_heads, L0_gnn_W_out, L0_gnn_a_out, L0_gnn_w1, L0_gnn_b1, L0_gnn_w2, L0_gnn_b2, L0_gnn_ln_gamma, L0_gnn_ln_beta, L1_gnn_W, L1_gnn_b):
    import jax
    import jax.numpy as jnp

    def _L0_gnn_ref(enc_inputs, adj, W_heads, a_heads, W_out, a_out, w1, b1, w2, b2, ln_gamma, ln_beta):
        import jax, jax.numpy as jnp
        import numpy as np
        LEAKY_ALPHA = 0.01
        NEG_INF = -1000000000.0
        LN_EPS = 1e-05

        def _gat_heads(x, adj, W, a):
            O = W.shape[-1]
            Wh = jnp.einsum('bnf,hfo->bhno', x, W)
            f1 = jnp.einsum('bhno,ho->bhn', Wh, a[:, :O])
            f2 = jnp.einsum('bhno,ho->bhn', Wh, a[:, O:])
            e = f1[:, :, :, None] + f2[:, :, None, :]
            e = jnp.where(e > 0, e, LEAKY_ALPHA * e)
            e = jnp.where(adj[None, None] > 0, e, NEG_INF)
            attn = jax.nn.softmax(e, axis=-1)
            return jnp.einsum('bhnm,bhmo->bhno', attn, Wh)
        B, N, _ = enc_inputs.shape
        h = jax.nn.elu(_gat_heads(enc_inputs, adj, W_heads, a_heads))
        h = jnp.transpose(h, (0, 2, 1, 3)).reshape(B, N, -1)
        out = _gat_heads(h, adj, W_out[None], a_out[None])[:, 0]
        out = jax.nn.elu(out)
        ffn = jnp.maximum(out @ w1 + b1, 0.0) @ w2 + b2
        y = ffn + out
        mu = jnp.mean(y, axis=-1, keepdims=True)
        var = jnp.var(y, axis=-1, keepdims=True)
        return (y - mu) / jnp.sqrt(var + LN_EPS) * ln_gamma + ln_beta

    def _L1_gnn_ref(x, adj, W, b):
        import jax, jax.numpy as jnp
        import numpy as np
        B, K, DIN, DOUT = (32, 64, 256, 256)
        Din = x.shape[-1]
        Wi, Wj = (W[:, :Din], W[:, Din:])
        mi = jnp.einsum('bkd,od->bko', x, Wi)
        mj = jnp.einsum('bkd,od->bko', x, Wj)
        a = adj.astype(x.dtype)
        deg = a.sum(axis=1)
        out = deg[None, :, None] * (mi + b) + jnp.einsum('ij,bjo->bio', a, mj)
        return out
    h = jnp.maximum(_layernorm(x, axis=-1), 0.0)
    x = x + _L0_gnn_ref(h, adj, L0_gnn_W_heads, L0_gnn_a_heads, L0_gnn_W_out, L0_gnn_a_out, L0_gnn_w1, L0_gnn_b1, L0_gnn_w2, L0_gnn_b2, L0_gnn_ln_gamma, L0_gnn_ln_beta)
    h = jnp.maximum(_layernorm(x, axis=-1), 0.0)
    x = x + _L1_gnn_ref(h, adj, L1_gnn_W, L1_gnn_b)
    return x

_drawn_inputs = setup_inputs


def setup_inputs(seed=0):
    import zlib

    import numpy as np

    out = dict(_drawn_inputs(seed))
    spreads = {'L0_gnn_b1': (0.0, 0.1),
     'L0_gnn_b2': (0.0, 0.1),
     'L0_gnn_ln_gamma': (1.0, 0.2),
     'L0_gnn_ln_beta': (0.0, 0.1)}
    factors = {}
    for name, (base, spread) in spreads.items():
        noise = np.random.default_rng([zlib.crc32(name.encode()), seed]).standard_normal(out[name].shape)
        drawn = base * np.exp(spread * noise) if base else spread * noise
        out[name] = jnp.asarray(drawn.astype(out[name].dtype))
    for name, factor in factors.items():
        out[name] = (out[name] * factor).astype(out[name].dtype)
    return out
```

```python
from contextlib import ExitStack

import concourse.bass as bass
from concourse import mybir

F32 = mybir.dt.float32
F32R = mybir.dt.float32r
BF16 = mybir.dt.bfloat16
I32 = mybir.dt.int32
ALU = mybir.AluOpType
ACT = mybir.ActivationFunctionType
AX = mybir.AxisListType

P = 128
SLOPE = 0.01
EPS = 1e-5
MASKED = -float(2 ** 100)
OUT = "out"
UNITS = [0, 1, OUT, 2, 3]
TR, GA, OT, AC = (0, 1), (2, 3), (4, 5), (6, 7)

PROLOGUE = [("hT", "ahead", TR), ("feat", "ahead", GA), ("row0", "ahead", GA[:1]), ("proj0", "ahead", (3, 2)),
            ("proj1", "ahead", (3, 2)), ("row1", "ahead", GA[1:])]
ITERATION = [("tr0", "heads", TR + TR), ("featout", "behind", GA[:1]), ("rowout", "behind", GA[1:]),
             ("proj2", "heads", GA), ("tr1", "heads", TR + TR), ("row2", "heads", GA[:1]),
             ("proj3", "heads", (3, 2)), ("trout", "behind", TR + TR), ("row3", "heads", GA[1:]),
             ("tr2", "heads", TR + TR), ("ffn1", "behind", GA), ("tr3", "heads", TR + TR),
             ("hT", "ahead", TR), ("feat", "ahead", GA), ("row0", "ahead", GA[:1]),
             ("ffn2", "behind", (3, 2)), ("proj0", "ahead", (3, 2)), ("h3T", "behind", TR),
             ("proj1", "ahead", (3, 2)), ("row1", "ahead", GA[1:]), ("lin", "behind", GA + GA),
             ("msg", "behind", GA)]


def banks(steps, who):
    at, last = {}, {}
    for step, whose, taken in steps:
        for n, bank in enumerate(taken):
            if whose in who:
                at[step, n] = (bank, last.get(bank))
                last[bank] = (step, n)
    return at


def gnn_kernel(nc, x, adj, W_heads, a_heads, W_out, a_out, w1, b1, w2, b2, ln_gamma, ln_beta, W_msg, b_msg, out):
    NB, N, F = x.shape
    H, _, O = W_heads.shape
    NT, KC, HC = N // P, F // P, H * O // P
    LAST = NB


    def unit(u, i):
        if isinstance(i, int) and i == 0:
            return u
        if isinstance(i, int) and i == NB:
            return len(UNITS) * i - 1
        return len(UNITS) * i - 1 + UNITS.index(u)

    ctx = ExitStack()
    with ctx:
        def sb(name, shape, dt=F32):
            return ctx.enter_context(nc.sbuf_tensor(name, shape, dt))

        def sem(name):
            return ctx.enter_context(nc.semaphore(name))

        def pair(name, shape):
            return sb(name + "_hi", shape, F32R), sb(name + "_lo", shape, F32R)

        ident = sb("ident", [P, P])
        ident_r = sb("ident_r", [P, P], F32R)
        Wp = pair("Wp", [P, KC, H * O])
        Wa = pair("Wa", [P, KC, 2 * H])
        Wo = pair("Wo", [P, HC, O])
        F1 = pair("F1", [P, KC, O])
        F2 = pair("F2", [P, KC, O])
        WmT = pair("WmT", [P, KC, 2 * O])
        adjT = pair("adjT", [P, NT, N])
        mask = sb("mask", [P, NT, N], BF16)
        deg = sb("deg", [P, NT])
        degb = sb("degb", [P, NT, O])
        gamma = sb("gamma", [P, O])
        beta = sb("beta", [P, O])
        b2row = sb("b2row", [P, O])
        aout = sb("aout", [P, 2 * O])
        b1col = sb("b1col", [P, KC])
        rsq = sb("rsq", [P, NT])
        pick = sb("pick", [64, 5, P], F32R)
        xa = sb("xa", [P, NT, F])
        hT = pair("hT", [P, KC, N])
        feat = sb("feat", [2 * H, N])
        featrow = sb("featrow", [64, N], F32R)
        f1col = sb("f1col", [P, NT, 2 * H])
        f1neg = sb("f1neg", [P, NT, H])
        row = sb("row", [P, N])
        q = sb("q", [P, NT, N])
        p = sb("p", [P, NT, N])
        g = sb("g", [P, NT])
        s = sb("s", [P, NT])
        m = sb("m", [P, NT])
        nb = sb("nb", [P, NT])
        rsum = sb("rsum", [P, NT])
        rinv = sb("rinv", [P, NT])
        pT = pair("pT", [P, NT, N])
        Wh = pair("Wh", [P, 2, NT, O])
        yb = sb("yb", [P, KC, N])
        h2 = [pair(f"h2_{k}", [P, KC, N]) for k in range(2)]
        xb = sb("xb", [P, NT, F])
        WM = pair("WM", [P, NT, O])
        oh = pair("oh", [P, KC, N])
        r = pair("r", [P, KC, N])
        y = sb("y", [P, NT, O])
        x2 = sb("x2", [P, NT, O])
        fo = sb("fo", [P, NT, 2])
        foneg = sb("foneg", [P, NT])
        forow = sb("forow", [64, N], F32R)
        junk = sb("junk", [P, 2, O])
        wa = sb("wa", [P, KC, 2 * H])
        stats = [sb(f"stats{k}", [P, NT, 6]) for k in range(3)]
        mv = [sb(f"mv{k}", [P, NT, 2]) for k in range(3)]
        ve = [sb(f"ve{k}", [P, NT]) for k in range(3)]
        rstd = [sb(f"rstd{k}", [P, NT]) for k in range(3)]
        ps = [ctx.enter_context(nc.psum_tensor(f"bank{k}", [P, 512], F32)) for k in range(8)]

        ld_adj, ld_heads, ld_const, ld_wout, ld_ffn = (sem(k) for k in ("ld_adj", "ld_heads", "ld_const", "ld_wout", "ld_ffn"))
        ids_step = sem("ids_step")
        passed = sem("passed")
        ids_made = sem("ids_made")
        step = sem("step")
        adj_float = sem("adj_float")
        heads_taken = sem("heads_taken")
        avec_taken = sem("avec_taken")
        setT = sem("setT")
        setT_used = sem("setT_used")
        weights_set = sem("weights_set")
        u_row, u_rowc = sem("u_row"), sem("u_rowc")
        u_q = sem("u_q")
        u_s, u_m = sem("u_s"), sem("u_m")
        u_w, u_l = sem("u_w"), sem("u_l")
        u_e, u_r, u_n = sem("u_e"), sem("u_r"), sem("u_n")
        u_tr, u_hi, u_lo = sem("u_tr"), sem("u_hi"), sem("u_lo")
        u_at = sem("u_at")
        u_E, u_E1, u_y = sem("u_E"), sem("u_E1"), sem("u_y")
        u_yh, u_yl = sem("u_yh"), sem("u_yl")
        ln_sum = [sem(f"ln_sum{k}") for k in range(3)]
        ln_mv = [sem(f"ln_mv{k}") for k in range(3)]
        ln_ve = [sem(f"ln_ve{k}") for k in range(3)]
        ln_rs = [sem(f"ln_rs{k}") for k in range(3)]
        a_x, a_h = sem("a_x"), sem("a_h")
        a_T, a_Th, a_Tl = sem("a_T"), sem("a_Th"), sem("a_Tl")
        a_f, a_fe, a_fh, a_fl = sem("a_f"), sem("a_fe"), sem("a_fh"), sem("a_fl")
        a_c, a_cc, a_cn = sem("a_c"), sem("a_cc"), sem("a_cn")
        w_mm = [sem("w_mm01"), sem("w_mm23")]
        w_hi = [sem("w_hi01"), sem("w_hi23")]
        w_lo = [sem("w_lo01"), sem("w_lo23")]
        acc = sem("acc")
        b_x = sem("b_x")
        b_Wh, b_Wl = sem("b_Wh"), sem("b_Wl")
        b_junk, b_fo, b_fn = sem("b_junk"), sem("b_fo"), sem("b_fn")
        b_fT, b_fTh, b_fTl = sem("b_fT"), sem("b_fTh"), sem("b_fTl")
        b_1, b_r, b_rh, b_rl = sem("b_1"), sem("b_r"), sem("b_rh"), sem("b_rl")
        b_2, b_y = sem("b_2"), sem("b_y")
        b_xb, b_z, b_x2 = sem("b_xb"), sem("b_z"), sem("b_x2")
        b_xd, b_h3 = sem("b_xd"), sem("b_h3")
        b_T, b_Th, b_Tl = sem("b_T"), sem("b_Th"), sem("b_Tl")
        b_l, b_mh, b_ml, b_mi = sem("b_l"), sem("b_mh"), sem("b_ml"), sem("b_mi")
        b_g, b_o, b_out = sem("b_g"), sem("b_o"), sem("b_out")

        ALL = slice(None)

        def cols(k, w=P):
            return slice(k * w, (k + 1) * w)

        def cut(t, *ix):
            return t[0][ix], t[1][ix]

        def f32(ap):
            return ap.bitcast(F32)

        def wait_apart(eng, sem, value):
            eng.wait_ge(sem, value)
            if not isinstance(value, int):
                eng.sem_inc(passed, 1)

        def later(value):
            return not isinstance(value, int) or value > 0

        def program(eng, prologue, iteration):
            prologue()
            iteration(0, ("heads", "ahead"))
            iteration(1, ("heads", "ahead", "behind"))
            with eng.Fori(2, NB - 1) as i:
                iteration(i, ("heads", "ahead", "behind"))
            iteration(NB - 1, ("heads", "behind"))
            iteration(NB, ("behind",))

        BANK = {k: v[0] for steps in (PROLOGUE, ITERATION) for k, v in banks(steps, ("heads", "ahead", "behind")).items()}

        def psum(name, n):
            return ps[BANK[name, n]]

        def wflat(t):
            return t[:, :, :].rearrange("p t o -> p (t o)")

        heads_w = wflat(p).rearrange("p (k h o) -> p k h o", k=KC, h=H)
        wout_w = wflat(p).rearrange("p (k o) -> p k o", k=HC)
        avec = [wflat(x2).rearrange("p (h o) -> p h o", h=2), wflat(y).rearrange("p (h o) -> p h o", h=2)]
        msg_w = xb[:, :, :].rearrange("p (t k) o -> p t (k o)", t=KC)
        relu_y = wflat(y).rearrange("p (k n) -> p k n", k=KC)
        pick_f = yb[0:64, :, :].rearrange("p k n -> p (k n)")[:, 0:5 * P].rearrange("p (s n) -> p s n", s=5)

        def outputs(u):
            return oh if u == OUT else h2[u % 2]

        def scalars(u):
            if u == OUT:
                return fo[:, :, 0], foneg[:, :]
            return f1col[:, :, u], f1neg[:, :, u]

        block = ctx.enter_context(nc.Block())

        @block.sync
        def _(sp):
            def prologue():
                sp.dma_start(wflat(q).bitcast(I32).rearrange("p (t n) -> p t n", t=NT),
                             adj.rearrange("(t p) j -> p t j", p=P)).then_inc(ld_adj, 16)
                sp.dma_start(xa[:, :, :], x[0].rearrange("(t p) f -> p t f", p=P)).then_inc(a_x, 16)
                for h in range(H):
                    sp.dma_start(heads_w[:, :, h, :], W_heads[h].rearrange("(k p) o -> p k o", p=P)).then_inc(ld_heads, 16)
                for k in range(2):
                    sp.dma_start(avec[k], a_heads[2 * k:2 * k + 2, :].partition_broadcast(P)).then_inc(ld_const, 16)
                sp.dma_start(aout[:, :], a_out.partition_broadcast(P)).then_inc(ld_const, 16)
                for dst, src in ((gamma[:, :], ln_gamma), (beta[:, :], ln_beta), (b2row[:, :], b2), (junk[:, 0, :], b_msg)):
                    sp.dma_start(dst, src.partition_broadcast(P)).then_inc(ld_const, 16)
                sp.dma_start(b1col[:, :], b1.rearrange("(k p) -> p k", p=P), allow_slow_non_contiguous=True).then_inc(ld_const, 16)
                sp.dma_start(msg_w, W_msg.rearrange("(t p) n -> p t n", p=P)).then_inc(ld_const, 16)
                sp.wait_ge(heads_taken, 1)
                sp.dma_start(wout_w, W_out.rearrange("(k p) o -> p k o", p=P)).then_inc(ld_wout, 16)
                sp.wait_ge(avec_taken, 1)
                for k, w in enumerate((w1, w2)):
                    sp.dma_start(y[:, KC * k:KC * (k + 1), :], w.rearrange("(k p) o -> p k o", p=P)).then_inc(ld_ffn, 16)
                sp.wait_ge(setT, NT + KC)

            def iteration(i, now):
                if "ahead" in now:
                    sp.wait_ge(a_T, KC * i + KC)
                    sp.dma_start(xa[:, :, :], x[i + 1].rearrange("(t p) f -> p t f", p=P)).then_inc(a_x, 16)
                if "behind" in now:
                    c = i - 1
                    if later(c):
                        sp.wait_ge(b_out, 16 * c)
                    sp.dma_start(xb[:, :, :], x[c].rearrange("(t p) f -> p t f", p=P)).then_inc(b_x, 16)
                    sp.wait_ge(b_o, 2 * c + 2)
                    sp.dma_start(out[c].rearrange("(t p) f -> p t f", p=P), xb[:, :, :]).then_inc(b_out, 16)

            program(sp, prologue, iteration)
            sp.wait_ge(b_out, 16 * NB)

        @block.tensor
        def _(pe):
            mm, tp = nc.tensor.matmul, nc.tensor.transpose
            place = {"now": None, "at": None}

            def read(name, n, i):
                b, c, nxt = i, (None if i is None else i - 1), (0 if i is None else i + 1)
                if name[:2] == "tr":
                    u = OUT if name == "trout" else int(name[2:])
                    return u_lo, NT * unit(u, i) + n + 1
                if name[:3] == "row":
                    u = OUT if name == "rowout" else int(name[3:])
                    return u_rowc, (unit(u, nxt) if u in (0, 1) else unit(u, i)) + 1
                if name[:4] == "proj":
                    h = int(name[4:])
                    return w_lo[h // 2], 4 * (nxt if h < 2 else b) + 2 * (h % 2) + n + 1
                return {"hT": (a_Tl, lambda: KC * nxt + n + 1), "feat": ((a_fh, a_cc)[n % 2], lambda: nxt + 1),
                        "featout": (b_fTl, lambda: c + 1), "ffn1": (b_r, lambda: KC * c + n + 1),
                        "ffn2": (b_y, lambda: 2 * c + n + 1), "h3T": (b_Tl, lambda: KC * c + n + 1),
                        "lin": (b_mi, lambda: NT * c + n + 1), "msg": (b_o, lambda: 2 * c + n + 1)}[name]

            def bank(i, name, n):
                k, last = place["at"][name, n]
                if last is not None:
                    done, value = read(*last, i)
                    pe.wait_ge(done, value() if callable(value) else value)
                elif i is None:
                    pe.wait_ge(setT_used, NT + KC)
                elif k in TR:
                    if "heads" in place["now"]:
                        pe.wait_ge(a_Tl, KC * i + KC)
                    if not isinstance(i, int) or i > 1:
                        pe.wait_ge(b_Tl, KC * (i - 1))
                else:
                    if "heads" in place["now"]:
                        pe.wait_ge(u_rowc, unit(1, i) + 1)
                        pe.wait_ge(w_lo[0], 4 * i + 4)
                    if not isinstance(i, int) or i > 1:
                        pe.wait_ge(b_mi, NT * (i - 1))
                        pe.wait_ge(b_o, 2 * (i - 1))
                return ps[k]

            def split3(to, lhs, rhs, first, last):
                mm(to, lhs[0], rhs[0], start=first, stop=False, skip_group_check=True)
                mm(to, lhs[0], rhs[1], start=False, stop=False, skip_group_check=True)
                return mm(to, lhs[1], rhs[0], start=False, stop=last, skip_group_check=True)

            def make_hT(i, b):
                pe.wait_ge(a_h, b + 1)
                for k in range(KC):
                    to = bank(i, "hT", k)
                    for t in range(NT):
                        last = tp(to[:, cols(t)], xa[:, t, cols(k)], ident[:, :])
                    last.then_inc(a_T, 1)

            def features(i, b):
                pe.wait_ge(a_Tl, KC * b + KC)
                to = bank(i, "feat", 0)
                for k in range(KC):
                    last = split3(to[0:2 * H, :], cut(Wa, ALL, k), cut(hT, ALL, k), k == 0, k == KC - 1)
                last.then_inc(a_f, 1)
                to = bank(i, "feat", 1)
                wait_apart(pe, a_fe, b + 1)
                for t in range(NT):
                    last = tp(to[:, cols(t, 2 * H)], feat[:, cols(t)], ident[0:2 * H, 0:2 * H])
                last.then_inc(a_c, 1)

            def spread(i, b, u):
                if u == OUT:
                    pe.wait_ge(b_fTl, b + 1)
                    pe.wait_ge(b_fTh, b + 1)
                    to = bank(i, "rowout", 0)
                    mm(to[:, :], pick[:, 0, :], forow[:, :], start=True, stop=True).then_inc(u_row, 1)
                else:
                    pe.wait_ge(a_fl, b + 1)
                    pe.wait_ge(a_fh, b + 1)
                    to = bank(i, f"row{u}", 0)
                    mm(to[:, :], pick[:, 1 + u, :], featrow[:, :], start=True, stop=True).then_inc(u_row, 1)

            def project(i, b, h):
                for half in range(2):
                    to = bank(i, f"proj{h}", half)
                    for tt in range(2):
                        for k in range(KC):
                            last = split3(to[:, cols(tt, O)], cut(hT, ALL, k, cols(2 * half + tt)),
                                          cut(Wp, ALL, k, cols(h, O)), k == 0 and tt == 0, k == KC - 1)
                    last.then_inc(w_mm[h // 2], 1)

            def transposes(i, u):
                n = unit(u, i)
                pe.wait_ge(u_n, NT * n + NT)
                for jt in range(NT):
                    to = bank(i, f"tr{u}", jt)
                    for t in range(NT):
                        last = tp(to[:, cols(t)], p[:, t, cols(jt)], ident[:, :])
                    last.then_inc(u_tr, 1)

            def attention(i, b, u):
                n = unit(u, i)
                if u == OUT:
                    pe.wait_ge(b_Wl, 2 * b + 2)
                else:
                    pe.wait_ge(w_lo[u // 2], 4 * b + 2 * (u % 2) + 2)
                for jt in range(NT):
                    pe.wait_ge(u_lo, NT * n + jt + 1)
                    for ot in range(KC):
                        if jt == 0 and later(n):
                            pe.wait_ge(u_y, KC * (n - 1) + ot + 1)
                        val = cut(WM, ALL, jt, cols(ot)) if u == OUT else cut(Wh, ALL, u % 2, jt, cols(ot))
                        last = split3(ps[OT[ot]][:, :], val, cut(pT, ALL, jt), jt == 0, jt == NT - 1)
                    last.then_inc(u_at, 1)

            def out_project(n, h, b):
                pe.wait_ge(u_yl, KC * n + KC)
                for half in range(2):
                    if h == 0 and later(b):
                        pe.wait_ge(b_fo, b)
                    for tt in range(2):
                        for k in range(KC):
                            last = split3(ps[AC[half]][:, cols(tt, O)], cut(h2[h % 2], ALL, k, cols(2 * half + tt)),
                                          cut(Wo, ALL, KC * h + k), h == 0 and k == 0 and tt == 0,
                                          h == H - 1 and k == KC - 1)
                last.then_inc(acc, 1)

            def out_features(i, c):
                pe.wait_ge(b_fo, c + 1)
                to = bank(i, "featout", 0)
                for t in range(NT):
                    last = tp(to[0:2, cols(t)], fo[:, t, :], ident[:, :])
                last.then_inc(b_fT, 1)

            def ffn_up(i, c):
                pe.wait_ge(u_yl, KC * unit(OUT, i) + KC)
                for dt in range(KC):
                    to = bank(i, "ffn1", dt)
                    for k in range(KC):
                        last = split3(to[:, :], cut(F1, ALL, k, cols(dt)), cut(oh, ALL, k), k == 0, k == KC - 1)
                    last.then_inc(b_1, 1)

            def ffn_down(i, c):
                pe.wait_ge(b_rl, KC * c + KC)
                for half in range(2):
                    to = bank(i, "ffn2", half)
                    for tt in range(2):
                        t = 2 * half + tt
                        for k in range(KC):
                            split3(to[:, cols(tt, O)], cut(r, ALL, k, cols(t)), cut(F2, ALL, k), k == 0 and tt == 0, False)
                        for k in range(KC):
                            for part in oh:
                                last = mm(to[:, tt * O + k * P:tt * O + (k + 1) * P], part[:, k, cols(t)], ident_r[:, :],
                                          start=False, stop=part is oh[1], skip_group_check=True)
                    last.then_inc(b_2, 1)

            def make_h3T(i, c):
                pe.wait_ge(b_h3, c + 1)
                for k in range(KC):
                    to = bank(i, "h3T", k)
                    for t in range(NT):
                        last = tp(to[:, cols(t)], y[:, t, cols(k)], ident[:, :])
                    last.then_inc(b_T, 1)

            def messages(i, c):
                pe.wait_ge(b_Tl, KC * c + KC)
                for t in range(NT):
                    to = bank(i, "lin", t)
                    for k in range(KC):
                        last = split3(to[:, :], cut(oh, ALL, k, cols(t)), cut(WmT, ALL, k), k == 0, k == KC - 1)
                    last.then_inc(b_l, 1)

            def gather(i, c):
                pe.wait_ge(b_ml, NT * c + NT)
                for half in range(2):
                    to = bank(i, "msg", half)
                    for tt in range(2):
                        for jt in range(NT):
                            last = split3(to[:, cols(tt, O)], cut(adjT, ALL, jt, cols(2 * half + tt)), cut(WM, ALL, jt),
                                          jt == 0 and tt == 0, jt == NT - 1)
                    last.then_inc(b_g, 1)

            def prologue():
                pe.wait_ge(ids_made, 3)
                pe.wait_ge(adj_float, 1)
                for jt in range(NT):
                    if jt >= 2:
                        pe.wait_ge(setT_used, jt - 1)
                    for t in range(NT):
                        last = tp(ps[jt % 2][:, cols(t)], q[:, t, cols(jt)], ident[:, :])
                    last.then_inc(setT, 1)
                pe.wait_ge(ld_const, 16 * 9)
                for k in range(KC):
                    pe.wait_ge(setT_used, NT - 1 + k)
                    for half in range(2):
                        for ot in range(KC):
                            last = tp(ps[k][:, half * O + ot * P:half * O + (ot + 1) * P],
                                      msg_w[:, ot, half * F + k * P:half * F + (k + 1) * P], ident[:, :])
                    last.then_inc(setT, 1)
                pe.wait_ge(weights_set, 1)
                place["now"], place["at"] = ("ahead",), banks(PROLOGUE, ("ahead",))
                make_hT(None, 0)
                features(None, 0)
                spread(None, 0, 0)
                project(None, 0, 0)
                project(None, 0, 1)
                spread(None, 0, 1)

            def iteration(i, now):
                heads, ahead, behind = ("heads" in now), ("ahead" in now), ("behind" in now)
                place["now"], place["at"] = now, banks(ITERATION, now)
                b, c = i, i - 1
                if heads:
                    transposes(i, 0)
                if behind:
                    out_project(len(UNITS) * i - 2, 3, c)
                if heads:
                    attention(i, b, 0)
                if behind:
                    out_features(i, c)
                    spread(i, c, OUT)
                if heads:
                    project(i, b, 2)
                    transposes(i, 1)
                    out_project(unit(0, i), 0, b)
                    attention(i, b, 1)
                    spread(i, b, 2)
                    project(i, b, 3)
                if behind:
                    transposes(i, OUT)
                if heads:
                    out_project(unit(1, i), 1, b)
                if behind:
                    attention(i, c, OUT)
                if heads:
                    spread(i, b, 3)
                    transposes(i, 2)
                    attention(i, b, 2)
                if behind:
                    ffn_up(i, c)
                if heads:
                    out_project(unit(2, i), 2, b)
                    transposes(i, 3)
                if ahead:
                    make_hT(i, b + 1)
                    features(i, b + 1)
                    spread(i, b + 1, 0)
                if behind:
                    ffn_down(i, c)
                if heads:
                    attention(i, b, 3)
                if ahead:
                    project(i, b + 1, 0)
                if behind:
                    make_h3T(i, c)
                if ahead:
                    project(i, b + 1, 1)
                    spread(i, b + 1, 1)
                if behind:
                    messages(i, c)
                    gather(i, c)

            program(pe, prologue, iteration)

        @block.scalar
        def _(act):
            def copy(out_ap, in_ap):
                return nc.scalar.activation(out_ap, in_ap, ACT.Copy)

            def split_hT(b):
                if later(b):
                    act.wait_ge(w_mm[1], 4 * b)
                for k in range(KC):
                    act.wait_ge(a_T, KC * b + k + 1)
                    nc.scalar.activation(hT[0][:, k, :], psum("hT", k)[:, :], ACT.Relu).then_inc(a_Th, 1)

            def feature_rows(b, last_unit):
                act.wait_ge(a_f, b + 1)
                if later(b):
                    act.wait_ge(a_c, b)
                    act.wait_ge(a_fl, b)
                copy(feat[:, :], psum("feat", 0)[0:2 * H, :]).then_inc(a_fe, 1)
                if later(b):
                    act.wait_ge(u_row, last_unit + 1)
                copy(featrow[0:2 * H, :], psum("feat", 0)[0:2 * H, :]).then_inc(a_fh, 1)
                act.wait_ge(a_c, b + 1)
                if later(b):
                    act.wait_ge(u_m, last_unit + 1)
                    act.wait_ge(a_cn, b)
                copy(f1col[:, :, :], psum("feat", 1)[:, 0:2 * H * NT].rearrange("p (t h) -> p t h", t=NT)).then_inc(a_cc, 1)

            def row_copy(n, u):
                act.wait_ge(u_row, n + 1)
                if later(n):
                    act.wait_ge(u_q, NT * n)
                copy(row[:, :], psum("rowout" if u == OUT else f"row{u}", 0)[:, :]).then_inc(u_rowc, 1)

            def values(b, h, user):
                if user is not None:
                    act.wait_ge(u_at, NT * user + NT)
                for half in range(2):
                    act.wait_ge(w_mm[h // 2], 4 * b + 2 * (h % 2) + half + 1)
                    copy(Wh[0][:, h % 2, cols(half, 2), :],
                         psum(f"proj{h}", half)[:, :].rearrange("p (t o) -> p t o", t=2)).then_inc(w_hi[h // 2], 1)

            def exps(n):
                act.wait_ge(u_m, n + 1)
                if later(n):
                    act.wait_ge(u_r, n)
                for t in range(NT):
                    act.wait_ge(u_l, NT * n + t + 1)
                    nc.scalar.activation(p[:, t, :], q[:, t, :], ACT.Exp, bias=nb[:, t:t + 1],
                                         accum_out=rsum[:, t:t + 1]).then_inc(u_e, 1)

            def prob_hi(n, u):
                for jt in range(NT):
                    act.wait_ge(u_tr, NT * n + jt + 1)
                    if later(n):
                        act.wait_ge(u_at, NT * (n - 1) + jt + 1)
                    copy(pT[0][:, jt, :], psum(f"tr{u}", jt)[:, :]).then_inc(u_hi, 1)

            def elu_exp(n):
                act.wait_ge(u_at, NT * n + NT)
                for ot in range(KC):
                    if later(n):
                        act.wait_ge(u_yl, KC * (n - 1) + ot + 1)
                    nc.scalar.activation(yb[:, ot, :], ps[OT[ot]][:, :], ACT.Exp).then_inc(u_E, 1)

            def out_values(c):
                act.wait_ge(acc, 4 * c + 4)
                if later(c):
                    act.wait_ge(b_g, 2 * c)
                for half in range(2):
                    copy(WM[0][:, cols(half, 2), :],
                         ps[AC[half]][:, :].rearrange("p (t o) -> p t o", t=2)).then_inc(b_Wh, 1)

            def out_rows(c, n):
                act.wait_ge(b_fT, c + 1)
                if later(c):
                    act.wait_ge(u_row, n)
                copy(forow[0:2, :], psum("featout", 0)[0:2, :]).then_inc(b_fTh, 1)

            def ffn_relu(c):
                if later(c):
                    act.wait_ge(b_T, KC * c)
                for dt in range(KC):
                    act.wait_ge(b_1, KC * c + dt + 1)
                    nc.scalar.activation(relu_y[:, dt, :], psum("ffn1", dt)[:, :], ACT.Relu,
                                         bias=b1col[:, dt:dt + 1]).then_inc(b_r, 1)

            def split_h3T(c):
                act.wait_ge(b_2, 2 * c + 2)
                for k in range(KC):
                    act.wait_ge(b_T, KC * c + k + 1)
                    nc.scalar.activation(oh[0][:, k, :], psum("h3T", k)[:, :], ACT.Relu).then_inc(b_Th, 1)

            def message_hi(c, n):
                act.wait_ge(u_at, NT * n + NT)
                for t in range(NT):
                    act.wait_ge(b_l, NT * c + t + 1)
                    copy(WM[0][:, t, :], psum("lin", t)[:, O:2 * O]).then_inc(b_mh, 1)

            def prologue():
                act.wait_ge(ld_const, 16 * 9)
                split_hT(0)
                act.wait_ge(ids_made, 5)
                feature_rows(0, None)
                row_copy(0, 0)
                values(0, 0, None)
                exps(0)
                values(0, 1, None)
                row_copy(1, 1)

            def iteration(i, now):
                heads, ahead, behind = ("heads" in now), ("ahead" in now), ("behind" in now)
                b, c = i, i - 1
                if heads:
                    prob_hi(unit(0, i), 0)
                if behind:
                    out_values(c)
                if heads:
                    exps(unit(1, i))
                    elu_exp(unit(0, i))
                if behind:
                    out_rows(c, unit(OUT, i))
                    row_copy(unit(OUT, i), OUT)
                if heads:
                    values(b, 2, unit(0, i))
                    prob_hi(unit(1, i), 1)
                if behind:
                    exps(unit(OUT, i))
                if heads:
                    elu_exp(unit(1, i))
                    row_copy(unit(2, i), 2)
                    values(b, 3, unit(1, i))
                if behind:
                    prob_hi(unit(OUT, i), OUT)
                if heads:
                    exps(unit(2, i))
                if behind:
                    elu_exp(unit(OUT, i))
                if heads:
                    row_copy(unit(3, i), 3)
                    prob_hi(unit(2, i), 2)
                    exps(unit(3, i))
                    elu_exp(unit(2, i))
                if behind:
                    ffn_relu(c)
                if heads:
                    prob_hi(unit(3, i), 3)
                if ahead:
                    split_hT(b + 1)
                    feature_rows(b + 1, unit(3, i))
                    row_copy(unit(0, i + 1), 0)
                if heads:
                    elu_exp(unit(3, i))
                if ahead:
                    values(b + 1, 0, unit(2, i))
                    exps(unit(0, i + 1))
                if behind:
                    split_h3T(c)
                if ahead:
                    values(b + 1, 1, unit(3, i))
                    row_copy(unit(1, i + 1), 1)
                if behind:
                    message_hi(c, unit(OUT, i))

            program(act, prologue, iteration)

        @block.vector
        def _(dve):
            tt, ts, stt = nc.vector.tensor_tensor, nc.vector.tensor_scalar, nc.vector.scalar_tensor_tensor

            def statistics(k, src, b):
                for t in range(NT):
                    last = nc.vector.bn_stats(stats[k][:, t, :], src[:, t, :])
                last.then_inc(ln_sum[k], 1)
                wait_apart(dve, ln_sum[k], b + 1)
                for t in range(NT):
                    last = nc.vector.bn_aggr(mv[k][:, t, :], stats[k][:, t, :])
                last.then_inc(ln_mv[k], 1)

            def normalise(k, to, src, b, done):
                dve.wait_ge(ln_rs[k], b + 1)
                for t in range(NT):
                    last = ts(to[:, t, :], src[:, t, :], mv[k][:, t, 0:1], rstd[k][:, t:t + 1], ALU.subtract, ALU.mult)
                last.then_inc(done, 1)

            def lo_hT(b):
                for k in range(KC):
                    dve.wait_ge(a_Th, KC * b + k + 1)
                    stt(hT[1][:, k, :], psum("hT", k)[:, :], 0.0, f32(hT[0][:, k, :]), ALU.max, ALU.subtract)\
                        .then_inc(a_Tl, 1)

            def feature_lo(b, last_unit):
                dve.wait_ge(a_fe, b + 1)
                dve.wait_ge(a_fh, b + 1)
                tt(featrow[32:32 + 2 * H, :], feat[:, :], f32(featrow[0:2 * H, :]), ALU.subtract).then_inc(a_fl, 1)
                dve.wait_ge(a_cc, b + 1)
                if later(b):
                    dve.wait_ge(u_w, NT * last_unit + NT)
                ts(f1neg[:, :, :], f1col[:, :, 0:H], -(1.0 - SLOPE), None, ALU.mult).then_inc(a_cn, 1)

            def masked(n, u):
                dve.wait_ge(u_rowc, n + 1)
                if later(n):
                    wait_apart(dve, u_e, NT * n)
                for t in range(NT):
                    nc.vector.tensor_tensor_reduce(out=q[:, t, :], in0=mask[:, t, :], in1=row[:, :], scale=1.0, scalar=-3e38,
                                                   op0=ALU.add, op1=ALU.max, accum_out=g[:, t:t + 1]).then_inc(u_q, 1)
                dve.wait_ge(u_q, NT * n + NT)
                f1, _ = scalars(u)
                tt(s[:, :], g[:, :], f1, ALU.add).then_inc(u_s, 1)
                dve.wait_ge(u_s, 2 * n + 1)
                stt(m[:, :], s[:, :], SLOPE, s[:, :], ALU.mult, ALU.max).then_inc(u_s, 1)
                dve.wait_ge(u_s, 2 * n + 2)
                tt(nb[:, :], f1, m[:, :], ALU.subtract).then_inc(u_m, 1)

            def leaky(n):
                for t in range(NT):
                    dve.wait_ge(u_w, NT * n + t + 1)
                    tt(q[:, t, :], q[:, t, :], p[:, t, :], ALU.max).then_inc(u_l, 1)

            def inverse(n):
                dve.wait_ge(u_e, NT * n + NT)
                if later(n):
                    dve.wait_ge(u_n, NT * n)
                nc.vector.reciprocal(rinv[:, :], rsum[:, :]).then_inc(u_r, 1)

            def prob_lo(n, u):
                for jt in range(NT):
                    dve.wait_ge(u_hi, NT * n + jt + 1)
                    tt(pT[1][:, jt, :], psum(f"tr{u}", jt)[:, :], f32(pT[0][:, jt, :]), ALU.subtract).then_inc(u_lo, 1)

            def elu(n):
                for ot in range(KC):
                    dve.wait_ge(u_E1, KC * n + ot + 1)
                    stt(yb[:, ot, :], yb[:, ot, :], 0.0, ps[OT[ot]][:, :], ALU.min, ALU.max).then_inc(u_y, 1)

            def values_lo(b, h):
                for half in range(2):
                    dve.wait_ge(w_hi[h // 2], 4 * b + 2 * (h % 2) + half + 1)
                    tt(Wh[1][:, h % 2, cols(half, 2), :], psum(f"proj{h}", half)[:, :].rearrange("p (t o) -> p t o", t=2),
                       f32(Wh[0][:, h % 2, cols(half, 2), :]), ALU.subtract).then_inc(w_lo[h // 2], 1)

            def out_values_lo(c):
                for half in range(2):
                    dve.wait_ge(b_Wh, 2 * c + half + 1)
                    tt(WM[1][:, cols(half, 2), :], ps[AC[half]][:, :].rearrange("p (t o) -> p t o", t=2),
                       f32(WM[0][:, cols(half, 2), :]), ALU.subtract).then_inc(b_Wl, 1)
                if later(c):
                    dve.wait_ge(b_fT, c)
                for t in range(NT):
                    for j in range(2):
                        k = 2 * t + j
                        if k >= 2:
                            dve.wait_ge(b_junk, 7 * c + k - 1)
                        last = nc.vector.tensor_tensor_reduce(
                            out=junk[:, j, :], in0=ps[AC[t // 2]][:, cols(t % 2, O)], in1=aout[:, cols(j, O)],
                            scale=1.0, scalar=0.0, op0=ALU.mult, op1=ALU.add, accum_out=fo[:, t, j:j + 1])
                        last.then_inc(b_junk if k < 7 else b_fo, 1)
                dve.wait_ge(b_fo, c + 1)
                ts(foneg[:, :], fo[:, :, 0], -(1.0 - SLOPE), None, ALU.mult).then_inc(b_fn, 1)

            def out_rows_lo(c):
                dve.wait_ge(b_fTh, c + 1)
                tt(forow[32:34, :], psum("featout", 0)[0:2, :], f32(forow[0:2, :]), ALU.subtract).then_inc(b_fTl, 1)

            def ffn_bias(c):
                dve.wait_ge(b_rl, KC * c + KC)
                for half in range(2):
                    dve.wait_ge(b_2, 2 * c + half + 1)
                    for t2 in range(2):
                        last = tt(y[:, 2 * half + t2, :], psum("ffn2", half)[:, cols(t2, O)], b2row[:, :], ALU.add)
                    last.then_inc(b_y, 1)
                dve.wait_ge(b_y, 2 * c + 2)
                statistics(1, y, c)

            def new_x(c):
                dve.wait_ge(ln_mv[1], c + 1)
                for t in range(NT):
                    last = stt(y[:, t, :], y[:, t, :], mv[1][:, t, 0:1], gamma[:, :], ALU.subtract, ALU.mult)
                last.then_inc(b_z, 1)
                dve.wait_ge(b_z, c + 1)
                dve.wait_ge(ln_rs[1], c + 1)
                dve.wait_ge(b_xb, c + 1)
                for t in range(NT):
                    last = stt(x2[:, t, :], y[:, t, :], rstd[1][:, t:t + 1], xb[:, t, :], ALU.mult, ALU.add)
                last.then_inc(b_x2, 1)
                dve.wait_ge(b_x2, c + 1)
                statistics(2, x2, c)

            def lo_h3T(c):
                for k in range(KC):
                    dve.wait_ge(b_Th, KC * c + k + 1)
                    stt(oh[1][:, k, :], psum("h3T", k)[:, :], 0.0, f32(oh[0][:, k, :]), ALU.max, ALU.subtract)\
                        .then_inc(b_Tl, 1)

            def message_lo(c):
                dve.wait_ge(b_xd, c + 1)
                for t in range(NT):
                    dve.wait_ge(b_mh, NT * c + t + 1)
                    tt(WM[1][:, t, :], psum("lin", t)[:, O:2 * O], f32(WM[0][:, t, :]), ALU.subtract).then_inc(b_ml, 1)
                    stt(xb[:, t, :], psum("lin", t)[:, 0:O], deg[:, t:t + 1], xb[:, t, :], ALU.mult, ALU.add)\
                        .then_inc(b_mi, 1)

            def result(c):
                for half in range(2):
                    dve.wait_ge(b_g, 2 * c + half + 1)
                    dve.wait_ge(b_mi, NT * c + 2 * half + 2)
                    tt(xb[:, cols(half, 2), :], psum("msg", half)[:, :].rearrange("p (t o) -> p t o", t=2),
                       xb[:, cols(half, 2), :], ALU.add).then_inc(b_o, 1)

            def prologue():
                steps = [0]

                def link(ins):
                    steps[0] += 1
                    ins.then_inc(step, 1)
                    dve.wait_ge(step, steps[0])

                def split(to, src):
                    link(nc.vector.tensor_copy(to[0], src))
                    return tt(to[1], src, f32(to[0]), ALU.subtract)

                dve.wait_ge(a_x, 16)
                statistics(0, xa, 0)
                dve.wait_ge(ld_adj, 16)
                ints = wflat(q).bitcast(I32)
                nc.vector.tensor_copy(wflat(q), ints).then_inc(adj_float, 1)
                dve.wait_ge(adj_float, 1)
                ts(wflat(mask), wflat(q), 0.0, MASKED, ALU.is_le, ALU.mult)
                link(nc.vector.reduce_sum(deg[:, :], q[:, :, :], axis=AX.X))
                normalise(0, xa, xa, 0, a_h)
                dve.wait_ge(ld_const, 16 * 9)
                for t in range(NT):
                    last = ts(degb[:, t, :], junk[:, 0, :], deg[:, t:t + 1], None, ALU.mult)
                link(last)
                for jt in range(NT):
                    dve.wait_ge(setT, jt + 1)
                    split(cut(adjT, ALL, jt), ps[jt % 2][:, :]).then_inc(setT_used, 1)
                for k in range(KC):
                    dve.wait_ge(setT, NT + k + 1)
                    split(cut(WmT, ALL, k), ps[k][:, :]).then_inc(setT_used, 1)
                dve.wait_ge(ld_heads, 16 * H)
                for k in range(KC):
                    for h in range(H):
                        for j in range(2):
                            link(nc.vector.tensor_tensor_reduce(
                                out=junk[:, j, :], in0=heads_w[:, k, h, :], in1=avec[h // 2][:, h % 2, cols(j, O)],
                                scale=1.0, scalar=0.0, op0=ALU.mult, op1=ALU.add,
                                accum_out=wa[:, k, j * H + h:j * H + h + 1]))
                nc.vector.memset(junk[:, 0, 0:1], 0.0).then_inc(avec_taken, 1)
                for k in range(KC):
                    link(split(cut(Wp, ALL, k), heads_w[:, k, :, :].rearrange("p h o -> p (h o)")))
                nc.vector.memset(junk[:, 1, 0:1], 0.0).then_inc(heads_taken, 1)
                link(split(cut(Wa, ALL), wa[:, :, :]))
                dve.wait_ge(ld_ffn, 32)
                link(split(cut(F1, ALL), y[:, 0:KC, :]))
                link(split(cut(F2, ALL), y[:, KC:2 * KC, :]))
                dve.wait_ge(ld_wout, 16)
                split(cut(Wo, ALL), wout_w).then_inc(weights_set, 1)
                lo_hT(0)
                feature_lo(0, None)
                masked(0, 0)
                values_lo(0, 0)
                leaky(0)
                inverse(0)
                values_lo(0, 1)
                masked(1, 1)

            def iteration(i, now):
                heads, ahead, behind = ("heads" in now), ("ahead" in now), ("behind" in now)
                b, c = i, i - 1
                if heads:
                    prob_lo(unit(0, i), 0)
                    leaky(unit(1, i))
                if behind:
                    out_values_lo(c)
                if heads:
                    inverse(unit(1, i))
                    elu(unit(0, i))
                if behind:
                    out_rows_lo(c)
                if heads:
                    values_lo(b, 2)
                if behind:
                    masked(unit(OUT, i), OUT)
                if heads:
                    prob_lo(unit(1, i), 1)
                if behind:
                    leaky(unit(OUT, i))
                    inverse(unit(OUT, i))
                if heads:
                    elu(unit(1, i))
                    masked(unit(2, i), 2)
                    values_lo(b, 3)
                if behind:
                    prob_lo(unit(OUT, i), OUT)
                if heads:
                    leaky(unit(2, i))
                    inverse(unit(2, i))
                if behind:
                    elu(unit(OUT, i))
                if heads:
                    masked(unit(3, i), 3)
                    prob_lo(unit(2, i), 2)
                if ahead:
                    dve.wait_ge(a_x, 16 * (b + 1) + 16)
                    statistics(0, xa, b + 1)
                if heads:
                    leaky(unit(3, i))
                    inverse(unit(3, i))
                    elu(unit(2, i))
                if ahead:
                    normalise(0, xa, xa, b + 1, a_h)
                if heads:
                    prob_lo(unit(3, i), 3)
                if ahead:
                    lo_hT(b + 1)
                    feature_lo(b + 1, unit(3, i))
                    masked(unit(0, i + 1), 0)
                if behind:
                    ffn_bias(c)
                if heads:
                    elu(unit(3, i))
                if ahead:
                    leaky(unit(0, i + 1))
                    values_lo(b + 1, 0)
                    inverse(unit(0, i + 1))
                if behind:
                    new_x(c)
                    normalise(2, y, x2, c, b_h3)
                    lo_h3T(c)
                if ahead:
                    values_lo(b + 1, 1)
                    masked(unit(1, i + 1), 1)
                if behind:
                    message_lo(c)
                    result(c)

            program(dve, prologue, iteration)

        @block.gpsimd
        def _(pool):
            tt, ts = nc.gpsimd.tensor_tensor, nc.gpsimd.tensor_scalar

            def deviation(k, b):
                wait_apart(pool, ln_mv[k], b + 1)
                ts(ve[k][:, :], mv[k][:, :, 1], 1.0, EPS, ALU.mult, ALU.add).then_inc(ln_ve[k], 1)
                pool.wait_ge(ln_ve[k], b + 1)
                tt(rstd[k][:, :], ve[k][:, :], rsq[:, :], ALU.pow).then_inc(ln_rs[k], 1)

            def other_slope(n, u):
                if later(n):
                    pool.wait_ge(u_tr, NT * n)
                _, f1n = scalars(u)
                for t in range(NT):
                    wait_apart(pool, u_q, NT * n + t + 1)
                    ts(p[:, t, :], q[:, t, :], SLOPE, f1n[:, t:t + 1], ALU.mult, ALU.add).then_inc(u_w, 1)

            def normalise_rows(n):
                wait_apart(pool, u_r, n + 1)
                for t in range(NT):
                    ts(p[:, t, :], p[:, t, :], rinv[:, t:t + 1], 1.0, ALU.mult, ALU.mult).then_inc(u_n, 1)

            def elu_parts(n, u, free):
                for ot in range(KC):
                    wait_apart(pool, u_E, KC * n + ot + 1)
                    ts(yb[:, ot, :], yb[:, ot, :], 1.0, -1.0, ALU.mult, ALU.add).then_inc(u_E1, 1)
                if free is not None:
                    pool.wait_ge(*free)
                to = outputs(u)
                for ot in range(KC):
                    wait_apart(pool, u_y, KC * n + ot + 1)
                    ts(to[0][:, ot, :], yb[:, ot, :], 1.0, 1.0, ALU.mult, ALU.mult).then_inc(u_yh, 1)
                for ot in range(KC):
                    pool.wait_ge(u_yh, KC * n + ot + 1)
                    tt(to[1][:, ot, :], yb[:, ot, :], f32(to[0][:, ot, :]), ALU.subtract).then_inc(u_yl, 1)

            def head_free(b, h):
                count = 4 * b + h - 1
                return (acc, count) if later(count) else None

            def relu_parts(c):
                if later(c):
                    pool.wait_ge(b_2, 2 * c)
                for dt in range(KC):
                    wait_apart(pool, b_r, KC * c + dt + 1)
                    ts(r[0][:, dt, :], relu_y[:, dt, :], 1.0, 1.0, ALU.mult, ALU.mult).then_inc(b_rh, 1)
                for dt in range(KC):
                    pool.wait_ge(b_rh, KC * c + dt + 1)
                    tt(r[1][:, dt, :], relu_y[:, dt, :], f32(r[0][:, dt, :]), ALU.subtract).then_inc(b_rl, 1)

            def add_beta(c):
                pool.wait_ge(b_x, 16 * c + 16)
                for t in range(NT):
                    last = tt(xb[:, t, :], xb[:, t, :], beta[:, :], ALU.add)
                last.then_inc(b_xb, 1)

            def add_degree_bias(c):
                pool.wait_ge(b_x2, c + 1)
                tt(xb[:, :, :], x2[:, :, :], degb[:, :, :], ALU.add).then_inc(b_xd, 1)

            def prologue():
                nc.gpsimd.memset(ident[:, :], 0.0).then_inc(ids_step, 1)
                nc.gpsimd.memset(pick_f, 0.0).then_inc(ids_step, 1)
                nc.gpsimd.memset(rsq[:, :], -0.5)
                pool.wait_ge(ids_step, 2)
                nc.gpsimd.affine_select(out=ident[:, :], in_=ident[:, :], compare_op=ALU.not_equal, fill=1.0, base=0,
                                        pattern=[[-1, P]], channel_multiplier=1).then_inc(ids_made, 1)
                for k, shift in enumerate((0, 32)):
                    nc.gpsimd.affine_select(out=pick_f[:, 0, :], in_=pick_f[:, 0, :], compare_op=ALU.not_equal, fill=1.0,
                                            base=-(1 + shift), pattern=[[0, P]], channel_multiplier=1)
                    nc.gpsimd.affine_select(out=pick_f[:, 1:5, :], in_=pick_f[:, 1:5, :], compare_op=ALU.not_equal, fill=1.0,
                                            base=-(H + shift), pattern=[[-1, H], [0, P]], channel_multiplier=1).then_inc(ids_step, 1)
                    pool.wait_ge(ids_step, 3 + k)
                wait_apart(pool, ids_made, 1)
                ts(ident_r[:, :], ident[:, :], 1.0, 1.0, ALU.mult, ALU.mult).then_inc(ids_made, 1)
                ts(pick[:, :, :], pick_f, 1.0, 1.0, ALU.mult, ALU.mult).then_inc(ids_made, 1)
                nc.gpsimd.memset(featrow[:, :].bitcast(F32), 0.0).then_inc(ids_made, 1)
                nc.gpsimd.memset(forow[:, :].bitcast(F32), 0.0).then_inc(ids_made, 1)
                pool.wait_ge(ids_made, 5)
                deviation(0, 0)
                other_slope(0, 0)
                normalise_rows(0)

            def iteration(i, now):
                heads, ahead, behind = ("heads" in now), ("ahead" in now), ("behind" in now)
                b, c = i, i - 1
                if heads:
                    other_slope(unit(1, i), 1)
                    normalise_rows(unit(1, i))
                    elu_parts(unit(0, i), 0, head_free(b, 0))
                if behind:
                    add_beta(c)
                    pool.wait_ge(b_fn, c + 1)
                    other_slope(unit(OUT, i), OUT)
                    normalise_rows(unit(OUT, i))
                if heads:
                    elu_parts(unit(1, i), 1, head_free(b, 1))
                    other_slope(unit(2, i), 2)
                    normalise_rows(unit(2, i))
                if behind:
                    elu_parts(unit(OUT, i), OUT, (b_l, NT * c) if later(c) else None)
                if heads:
                    other_slope(unit(3, i), 3)
                if ahead:
                    deviation(0, b + 1)
                if heads:
                    normalise_rows(unit(3, i))
                    elu_parts(unit(2, i), 2, head_free(b, 2))
                if behind:
                    relu_parts(c)
                if ahead:
                    pool.wait_ge(a_cn, b + 2)
                    other_slope(unit(0, i + 1), 0)
                if behind:
                    deviation(1, c)
                if heads:
                    elu_parts(unit(3, i), 3, head_free(b, 3))
                if ahead:
                    normalise_rows(unit(0, i + 1))
                if behind:
                    add_degree_bias(c)
                    deviation(2, c)

            program(pool, prologue, iteration)


_INS = ["x", "adj", "L0_gnn_W_heads", "L0_gnn_a_heads", "L0_gnn_W_out", "L0_gnn_a_out", "L0_gnn_w1", "L0_gnn_b1",
        "L0_gnn_w2", "L0_gnn_b2", "L0_gnn_ln_gamma", "L0_gnn_ln_beta", "L1_gnn_W", "L1_gnn_b"]


def kernel(**inputs):
    import numpy as _np
    import concourse.bacc as _bacc
    from concourse import mybir as _mybir
    from concourse.bass_utils import run_bass_kernel_spmd as _run

    nc = _bacc.Bacc("TRN2", target_bir_lowering=False, num_devices=1)
    arrays, args = {}, []
    for name in _INS:
        a = _np.ascontiguousarray(inputs[name])
        arrays[f"in_{name}"] = a
        args.append(nc.dram_tensor(f"in_{name}", a.shape, _mybir.dt.from_np(a.dtype), kind="ExternalInput").ap())
    shape = arrays["in_x"].shape
    args.append(nc.dram_tensor("out_0", shape, _mybir.dt.float32, kind="ExternalOutput").ap())
    gnn_kernel(nc, *args)
    got = _run(nc, [arrays], core_ids=[0])
    return got.results[0]["out_0"]
```

```python
from contextlib import ExitStack

import concourse.bass as bass
from concourse import mybir

F32 = mybir.dt.float32
F32R = mybir.dt.float32r
BF16 = mybir.dt.bfloat16
I32 = mybir.dt.int32
ALU = mybir.AluOpType
ACT = mybir.ActivationFunctionType
AX = mybir.AxisListType

P = 128
SLOPE = 0.01
EPS = 1e-5
MASKED = -float(2 ** 100)
OUT = "out"
SLOT = {1: 0, OUT: 1, 2: 2, 3: 0, 0: 1}
TR, GA, OT, AC = (0, 1), (2, 3), (4, 5), (6, 7)

PROLOGUE = [("hT", "ahead", TR), ("featrow", "ahead", (3,)), ("featcol", "ahead", (3,)), ("row0", "ahead", (2,)),
            ("proj0", "ahead", (2, 3)), ("row1", "ahead", (3,)), ("tr0", "ahead", TR + TR), ("proj1", "ahead", (2, 3)),
            ("tr1", "ahead", TR + TR), ("proj2", "ahead", (2, 3))]
ITERATION = [("row2", "heads", (3,)), ("proj3", "heads", (2, 3)), ("hT", "ahead", TR), ("trout", "behind", TR + TR),
             ("featrow", "ahead", (3,)), ("row3", "heads", (2,)), ("featcol", "ahead", (3,)),
             ("tr2", "heads", TR + TR), ("row0", "ahead", (2,)), ("tr3", "heads", TR + TR),
             ("ffn1", "behind", (3, 2)), ("row1", "ahead", (3,)), ("proj0", "ahead", (2, 3)),
             ("tr0", "ahead", TR + TR), ("ffn2", "behind", (2, 3)), ("proj1", "ahead", (2, 3)),
             ("tr1", "ahead", TR + TR), ("proj2", "ahead", (2, 3)), ("h3T", "behind", TR),
             ("featout", "heads", (2,)), ("lin", "behind", (3, 2, 3, 2)), ("rowout", "heads", (3,)),
             ("msg", "behind", (2, 3))]


def banks(steps, who):
    at, last = {}, {}
    for step, whose, taken in steps:
        for n, bank in enumerate(taken):
            if whose in who:
                at[step, n] = (bank, last.get(bank))
                last[bank] = (step, n)
    return at


def gnn_kernel(nc, x, adj, W_heads, a_heads, W_out, a_out, w1, b1, w2, b2, ln_gamma, ln_beta, W_msg, b_msg, out):
    NB, N, F = x.shape
    H, _, O = W_heads.shape
    NT, KC, HC = N // P, F // P, H * O // P
    LAST = NB


    def unit(u, b):
        if u == OUT:
            return 5 * NB - 1 if isinstance(b, int) and b == NB - 1 else 5 * b + 6
        if isinstance(b, int) and b == 0:
            return u
        return 5 * b + {0: -1, 1: 0, 2: 2, 3: 3}[u]

    def slot_before(u, b):
        first = isinstance(b, int) and b == 0
        if u == OUT:
            return unit(OUT, b - 1) if isinstance(b, int) and b == NB - 1 else unit(0, b + 1)
        if u == 0:
            return None if first else 0 if isinstance(b, int) and b == 1 else unit(OUT, b - 2)
        if u == 3:
            return unit(1, b)
        return None if first else unit({1: 3, 2: 2}[u], b - 1)

    ctx = ExitStack()
    with ctx:
        def sb(name, shape, dt=F32):
            return ctx.enter_context(nc.sbuf_tensor(name, shape, dt))

        def sem(name):
            return ctx.enter_context(nc.semaphore(name))

        def pair(name, shape):
            return sb(name + "_hi", shape, F32R), sb(name + "_lo", shape, F32R)

        ident = sb("ident", [P, P])
        ident_r = sb("ident_r", [P, P], F32R)
        Wp = pair("Wp", [P, KC, H * O])
        Wa = pair("Wa", [P, KC, 2 * H])
        Wo = pair("Wo", [P, HC, O])
        F1 = pair("F1", [P, KC, O])
        F2 = pair("F2", [P, KC, O])
        WmT = pair("WmT", [P, KC, 2 * O])
        adjT = pair("adjT", [P, NT, N])
        mask = sb("mask", [P, NT, N], BF16)
        deg = sb("deg", [P, NT])
        gamma = sb("gamma", [P, O])
        beta = sb("beta", [P, O])
        bias = sb("bias", [64, 2, O], F32R)
        aout = sb("aout", [P, 2 * O])
        b1col = sb("b1col", [P, KC])
        rsq = sb("rsq", [P, NT])
        pick = sb("pick", [64, 5, P], F32R)
        xa = sb("xa", [P, NT, F])
        hT = pair("hT", [P, KC, N])
        feat = sb("feat", [2 * H, N])
        featrow = sb("featrow", [64, N], F32R)
        f1col = sb("f1col", [P, NT, 2 * H])
        f1neg = sb("f1neg", [P, NT, H])
        row = sb("row", [P, N])
        q = sb("q", [P, NT, N])
        pp = [sb(f"p{k}", [P, NT, N]) for k in range(3)]
        g = sb("g", [P, NT])
        s = sb("s", [P, NT])
        m = sb("m", [P, NT])
        nb = sb("nb", [P, NT])
        rsum = sb("rsum", [P, NT])
        rinv = sb("rinv", [P, NT])
        pT = pair("pT", [P, NT, N])
        Wh = pair("Wh", [P, 2, NT, O])
        yb = sb("yb", [P, KC, N])
        h2 = pair("h2", [P, KC, N])
        xb = sb("xb", [P, NT, F])
        WM = pair("WM", [P, NT, O])
        M = pair("M", [P, NT, O])
        oh = pair("oh", [P, KC, N])
        y = sb("y", [P, NT, O])
        fo = sb("fo", [P, NT, 2])
        foneg = sb("foneg", [P, NT])
        forow = sb("forow", [64, N], F32R)
        junk = sb("junk", [P, O])
        stats = [sb(f"stats{k}", [P, NT, 6]) for k in range(3)]
        mv = [sb(f"mv{k}", [P, NT, 2]) for k in range(3)]
        ve = [sb(f"ve{k}", [P, NT]) for k in range(3)]
        rstd = [sb(f"rstd{k}", [P, NT]) for k in range(3)]
        ps = [ctx.enter_context(nc.psum_tensor(f"bank{k}", [P, 512], F32)) for k in range(8)]

        ld_adj, ld_heads, ld_const, ld_wout, ld_ffn = (sem(k) for k in ("ld_adj", "ld_heads", "ld_const", "ld_wout", "ld_ffn"))
        ids_step = sem("ids_step")
        passed = sem("passed")
        ids_made = sem("ids_made")
        step = sem("step")
        adj_float = sem("adj_float")
        heads_taken = sem("heads_taken")
        avec_taken = sem("avec_taken")
        setT = sem("setT")
        setT_used = sem("setT_used")
        weights_set = sem("weights_set")
        u_row, u_rowc = sem("u_row"), sem("u_rowc")
        u_q = sem("u_q")
        u_s, u_m = sem("u_s"), sem("u_m")
        u_w, u_l = sem("u_w"), sem("u_l")
        u_e, u_r, u_n = sem("u_e"), sem("u_r"), sem("u_n")
        u_tr, u_hi, u_lo = sem("u_tr"), sem("u_hi"), sem("u_lo")
        u_at = sem("u_at")
        u_E, u_E1, u_y = sem("u_E"), sem("u_E1"), sem("u_y")
        u_yh, u_yl = sem("u_yh"), sem("u_yl")
        ln_sum = [sem(f"ln_sum{k}") for k in range(3)]
        ln_mv = [sem(f"ln_mv{k}") for k in range(3)]
        ln_ve = [sem(f"ln_ve{k}") for k in range(3)]
        ln_rs = [sem(f"ln_rs{k}") for k in range(3)]
        a_x, a_h = sem("a_x"), sem("a_h")
        a_T, a_Th, a_Tl = sem("a_T"), sem("a_Th"), sem("a_Tl")
        a_f, a_fe, a_fh, a_fl = sem("a_f"), sem("a_fe"), sem("a_fh"), sem("a_fl")
        a_c, a_cc, a_cn = sem("a_c"), sem("a_cc"), sem("a_cn")
        w_mm = [sem("w_mm01"), sem("w_mm23")]
        w_hi = [sem("w_hi01"), sem("w_hi23")]
        w_lo = [sem("w_lo01"), sem("w_lo23")]
        acc = sem("acc")
        b_x = sem("b_x")
        b_Wh, b_Wl = sem("b_Wh"), sem("b_Wl")
        b_junk, b_fo, b_fn = sem("b_junk"), sem("b_fo"), sem("b_fn")
        b_fT, b_fTh, b_fTl = sem("b_fT"), sem("b_fTh"), sem("b_fTl")
        b_1, b_r, b_rh, b_rl = sem("b_1"), sem("b_r"), sem("b_rh"), sem("b_rl")
        b_2, b_y = sem("b_2"), sem("b_y")
        b_xb, b_z, b_x2 = sem("b_xb"), sem("b_z"), sem("b_x2")
        b_h3 = sem("b_h3")
        b_T, b_Th, b_Tl = sem("b_T"), sem("b_Th"), sem("b_Tl")
        b_l, b_mh, b_ml, b_mi = sem("b_l"), sem("b_mh"), sem("b_ml"), sem("b_mi")
        b_g, b_o, b_out = sem("b_g"), sem("b_o"), sem("b_out")

        ALL = slice(None)

        def cols(k, w=P):
            return slice(k * w, (k + 1) * w)

        def cut(t, *ix):
            return t[0][ix], t[1][ix]

        def f32(ap):
            return ap.bitcast(F32)

        def wait_apart(eng, sem, value):
            eng.wait_ge(sem, value)
            if not isinstance(value, int):
                eng.sem_inc(passed, 1)

        def later(value):
            return not isinstance(value, int) or value > 0

        def program(eng, prologue, iteration):
            prologue()
            iteration(0, ("heads", "ahead"))
            iteration(1, ("heads", "ahead", "behind"))
            with eng.Fori(2, NB - 1) as i:
                iteration(i, ("heads", "ahead", "behind"))
            iteration(NB - 1, ("heads", "behind"))
            iteration(NB, ("behind",))

        BANK = {k: v[0] for steps in (PROLOGUE, ITERATION) for k, v in banks(steps, ("heads", "ahead", "behind")).items()}

        def psum(name, n):
            return ps[BANK[name, n]]

        def wflat(t):
            return t[:, :, :].rearrange("p t o -> p (t o)")

        p = pp[0]
        heads_w = wflat(p).rearrange("p (k h o) -> p k h o", k=KC, h=H)
        wout_w = wflat(p).rearrange("p (k o) -> p k o", k=HC)
        avec = [wflat(pp[1])[:, 0:4 * O].rearrange("p (h o) -> p h o", h=2), wflat(y).rearrange("p (h o) -> p h o", h=2)]
        msg_w = xb[:, :, :].rearrange("p (t k) o -> p t (k o)", t=KC)
        bias_f = wflat(pp[1])[0:2, 4 * O:6 * O].rearrange("p (k o) -> p k o", k=2)
        r = [wflat(t).rearrange("p (k n) -> p k n", k=KC) for t in WM]
        wa = row[:, 0:KC * 2 * H].rearrange("p (k j) -> p k j", k=KC)
        relu_y = wflat(y).rearrange("p (k n) -> p k n", k=KC)
        pick_f = yb[0:64, :, :].rearrange("p k n -> p (k n)")[:, 0:5 * P].rearrange("p (s n) -> p s n", s=5)

        def outputs(u):
            return oh if u == OUT else h2

        def scalars(u):
            if u == OUT:
                return fo[:, :, 0], foneg[:, :]
            return f1col[:, :, u], f1neg[:, :, u]

        block = ctx.enter_context(nc.Block())

        @block.sync
        def _(sp):
            def prologue():
                sp.dma_start(wflat(q).bitcast(I32).rearrange("p (t n) -> p t n", t=NT),
                             adj.rearrange("(t p) j -> p t j", p=P)).then_inc(ld_adj, 16)
                sp.dma_start(xa[:, :, :], x[0].rearrange("(t p) f -> p t f", p=P)).then_inc(a_x, 16)
                for h in range(H):
                    sp.dma_start(heads_w[:, :, h, :], W_heads[h].rearrange("(k p) o -> p k o", p=P)).then_inc(ld_heads, 16)
                for k in range(2):
                    sp.dma_start(avec[k], a_heads[2 * k:2 * k + 2, :].partition_broadcast(P)).then_inc(ld_const, 16)
                sp.dma_start(aout[:, :], a_out.partition_broadcast(P)).then_inc(ld_const, 16)
                for dst, src in ((gamma[:, :], ln_gamma), (beta[:, :], ln_beta), (bias_f[:, 0, :], b2), (bias_f[:, 1, :], b_msg)):
                    sp.dma_start(dst, src.partition_broadcast(dst.shape[0])).then_inc(ld_const, 16)
                sp.dma_start(b1col[:, :], b1.rearrange("(k p) -> p k", p=P), allow_slow_non_contiguous=True).then_inc(ld_const, 16)
                sp.dma_start(msg_w, W_msg.rearrange("(t p) n -> p t n", p=P)).then_inc(ld_const, 16)
                sp.wait_ge(heads_taken, 1)
                sp.dma_start(wout_w, W_out.rearrange("(k p) o -> p k o", p=P)).then_inc(ld_wout, 16)
                sp.wait_ge(avec_taken, 1)
                for k, w in enumerate((w1, w2)):
                    sp.dma_start(y[:, KC * k:KC * (k + 1), :], w.rearrange("(k p) o -> p k o", p=P)).then_inc(ld_ffn, 16)
                sp.wait_ge(setT, NT + KC)

            def iteration(i, now):
                if "ahead" in now:
                    sp.wait_ge(a_T, KC * i + KC)
                    sp.dma_start(xa[:, :, :], x[i + 1].rearrange("(t p) f -> p t f", p=P)).then_inc(a_x, 16)
                if "behind" in now:
                    c = i - 1
                    if later(c):
                        sp.wait_ge(b_o, 2 * c)
                        sp.dma_start(out[c - 1].rearrange("(t p) f -> p t f", p=P), xb[:, :, :]).then_inc(b_out, 16)
                        sp.wait_ge(b_out, 16 * c)
                    sp.dma_start(xb[:, :, :], x[c].rearrange("(t p) f -> p t f", p=P)).then_inc(b_x, 16)

            program(sp, prologue, iteration)
            sp.wait_ge(b_o, 2 * NB)
            sp.dma_start(out[NB - 1].rearrange("(t p) f -> p t f", p=P), xb[:, :, :]).then_inc(b_out, 16)
            sp.wait_ge(b_out, 16 * NB)

        @block.tensor
        def _(pe):
            mm, tp = nc.tensor.matmul, nc.tensor.transpose
            place = {"now": None, "at": None}

            def read(name, n, i):
                b, c, nxt = i, (None if i is None else i - 1), (0 if i is None else i + 1)
                if name[:2] == "tr":
                    return u_lo, NT * (unit(OUT, c) if name == "trout" else unit(int(name[2:]), b if name[2:] in "23" else nxt)) + n + 1
                if name[:3] == "row":
                    return u_rowc, unit(OUT, b) + 1 if name == "rowout" else unit(int(name[3:]), b if name[3:] in "23" else nxt) + 1
                if name[:4] == "proj":
                    h = int(name[4:])
                    return w_lo[h // 2], 4 * (nxt if h < 3 else b) + 2 * (h % 2) + n + 1
                return {"hT": (a_Tl, lambda: KC * nxt + n + 1), "featrow": (a_fh, lambda: nxt + 1), "featcol": (a_cc, lambda: nxt + 1),
                        "featout": (b_fTl, lambda: b + 1), "ffn1": (b_r, lambda: KC * c + n + 1),
                        "ffn2": (b_y, lambda: 2 * c + n + 1), "h3T": (b_Tl, lambda: KC * c + n + 1),
                        "lin": (b_mi, lambda: NT * c + n + 1), "msg": (b_o, lambda: 2 * c + n + 1)}[name]

            def bank(i, name, n):
                k, last = place["at"][name, n]
                if last is not None:
                    done, value = read(*last, i)
                    pe.wait_ge(done, value() if callable(value) else value)
                elif i is None:
                    pe.wait_ge(setT_used, NT + KC)
                elif k in TR:
                    if "heads" in place["now"]:
                        pe.wait_ge(u_lo, NT * unit(1, i) + NT)
                    if not isinstance(i, int) or i > 1:
                        pe.wait_ge(b_Tl, KC * (i - 1))
                else:
                    if "heads" in place["now"]:
                        pe.wait_ge(u_rowc, unit(1, i) + 1)
                        pe.wait_ge(w_lo[0], 4 * i + 4)
                        pe.wait_ge(w_lo[1], 4 * i + 2)
                    if "behind" in place["now"]:
                        pe.wait_ge(u_rowc, unit(OUT, i - 1) + 1)
                    if not isinstance(i, int) or i > 1:
                        pe.wait_ge(b_mi, NT * (i - 1))
                        pe.wait_ge(b_o, 2 * (i - 1))
                return ps[k]

            def split3(to, lhs, rhs, first, last):
                mm(to, lhs[0], rhs[0], start=first, stop=False, skip_group_check=True)
                mm(to, lhs[0], rhs[1], start=False, stop=False, skip_group_check=True)
                return mm(to, lhs[1], rhs[0], start=False, stop=last, skip_group_check=True)

            def make_hT(i, b):
                pe.wait_ge(a_h, b + 1)
                for k in range(KC):
                    to = bank(i, "hT", k)
                    for t in range(NT):
                        last = tp(to[:, cols(t)], xa[:, t, cols(k)], ident[:, :])
                    last.then_inc(a_T, 1)

            def feature_rows(i, b):
                pe.wait_ge(a_Tl, KC * b + KC)
                to = bank(i, "featrow", 0)
                for k in range(KC):
                    last = split3(to[0:2 * H, :], cut(Wa, ALL, k), cut(hT, ALL, k), k == 0, k == KC - 1)
                last.then_inc(a_f, 1)

            def feature_columns(i, b):
                to = bank(i, "featcol", 0)
                wait_apart(pe, a_fe, b + 1)
                for t in range(NT):
                    last = tp(to[:, cols(t, 2 * H)], feat[:, cols(t)], ident[0:2 * H, 0:2 * H])
                last.then_inc(a_c, 1)

            def spread(i, b, u):
                if u == OUT:
                    pe.wait_ge(b_fTl, b + 1)
                    pe.wait_ge(b_fTh, b + 1)
                    to = bank(i, "rowout", 0)
                    mm(to[:, :], pick[:, 0, :], forow[:, :], start=True, stop=True).then_inc(u_row, 1)
                else:
                    pe.wait_ge(a_fl, b + 1)
                    pe.wait_ge(a_fh, b + 1)
                    to = bank(i, f"row{u}", 0)
                    mm(to[:, :], pick[:, 1 + u, :], featrow[:, :], start=True, stop=True).then_inc(u_row, 1)

            def project(i, b, h):
                for half in range(2):
                    to = bank(i, f"proj{h}", half)
                    for tt in range(2):
                        for k in range(KC):
                            last = split3(to[:, cols(tt, O)], cut(hT, ALL, k, cols(2 * half + tt)),
                                          cut(Wp, ALL, k, cols(h, O)), k == 0 and tt == 0, k == KC - 1)
                    last.then_inc(w_mm[h // 2], 1)

            def transposes(i, b, u, half):
                n, p = unit(u, b), pp[SLOT[u]]
                pe.wait_ge(u_n, NT * n + NT)
                for jt in (2 * half, 2 * half + 1):
                    to = bank(i, f"tr{u}", jt)
                    for t in range(NT):
                        last = tp(to[:, cols(t)], p[:, t, cols(jt)], ident[:, :])
                    last.then_inc(u_tr, 1)

            def attention(i, b, u):
                n = unit(u, b)
                if u == OUT:
                    pe.wait_ge(b_Wl, 2 * b + 2)
                else:
                    pe.wait_ge(w_lo[u // 2], 4 * b + 2 * (u % 2) + 2)
                for jt in range(NT):
                    pe.wait_ge(u_lo, NT * n + jt + 1)
                    for ot in range(KC):
                        if jt == 0 and later(n):
                            pe.wait_ge(u_y, KC * (n - 1) + ot + 1)
                        val = cut(WM, ALL, jt, cols(ot)) if u == OUT else cut(Wh, ALL, u % 2, jt, cols(ot))
                        last = split3(ps[OT[ot]][:, :], val, cut(pT, ALL, jt), jt == 0, jt == NT - 1)
                    last.then_inc(u_at, 1)

            def out_project(h, b):
                pe.wait_ge(u_yl, KC * unit(h, b) + KC)
                for half in range(2):
                    if h == 0 and later(b):
                        pe.wait_ge(b_fo, b)
                    for tt in range(2):
                        for k in range(KC):
                            last = split3(ps[AC[half]][:, cols(tt, O)], cut(h2, ALL, k, cols(2 * half + tt)),
                                          cut(Wo, ALL, KC * h + k), h == 0 and k == 0 and tt == 0,
                                          h == H - 1 and k == KC - 1)
                last.then_inc(acc, 1)

            def out_features(i, c):
                pe.wait_ge(b_fo, c + 1)
                to = bank(i, "featout", 0)
                for t in range(NT):
                    last = tp(to[0:2, cols(t)], fo[:, t, :], ident[:, :])
                last.then_inc(b_fT, 1)

            def ffn_up(i, c):
                pe.wait_ge(u_yl, KC * unit(OUT, c) + KC)
                for dt in range(KC):
                    to = bank(i, "ffn1", dt)
                    for k in range(KC):
                        last = split3(to[:, :], cut(F1, ALL, k, cols(dt)), cut(oh, ALL, k), k == 0, k == KC - 1)
                    last.then_inc(b_1, 1)

            def ffn_down(i, c):
                pe.wait_ge(b_rl, KC * c + KC)
                for half in range(2):
                    to = bank(i, "ffn2", half)
                    for tt in range(2):
                        t = 2 * half + tt
                        for k in range(KC):
                            split3(to[:, cols(tt, O)], cut(r, ALL, k, cols(t)), cut(F2, ALL, k), k == 0 and tt == 0, False)
                        for k in range(KC):
                            for part in oh:
                                mm(to[:, tt * O + k * P:tt * O + (k + 1) * P], part[:, k, cols(t)], ident_r[:, :],
                                   start=False, stop=False, skip_group_check=True)
                        last = mm(to[:, cols(tt, O)], pick[:, 0, :], bias[:, 0, :], start=False, stop=True, skip_group_check=True)
                    last.then_inc(b_2, 1)

            def make_h3T(i, c):
                pe.wait_ge(b_h3, c + 1)
                for k in range(KC):
                    to = bank(i, "h3T", k)
                    for t in range(NT):
                        last = tp(to[:, cols(t)], y[:, t, cols(k)], ident[:, :])
                    last.then_inc(b_T, 1)

            def messages(i, c):
                pe.wait_ge(b_Tl, KC * c + KC)
                for t in range(NT):
                    to = bank(i, "lin", t)
                    for k in range(KC):
                        split3(to[:, :], cut(oh, ALL, k, cols(t)), cut(WmT, ALL, k), k == 0, False)
                    mm(to[:, 0:O], pick[:, 0, :], bias[:, 1, :], start=False, stop=True, skip_group_check=True).then_inc(b_l, 1)

            def gather(i, c):
                pe.wait_ge(b_ml, NT * c + NT)
                for half in range(2):
                    to = bank(i, "msg", half)
                    for tt in range(2):
                        for jt in range(NT):
                            last = split3(to[:, cols(tt, O)], cut(adjT, ALL, jt, cols(2 * half + tt)), cut(M, ALL, jt),
                                          jt == 0 and tt == 0, jt == NT - 1)
                    last.then_inc(b_g, 1)

            def prologue():
                pe.wait_ge(ids_made, 3)
                pe.wait_ge(adj_float, 1)
                for jt in range(NT):
                    if jt >= 2:
                        pe.wait_ge(setT_used, jt - 1)
                    for t in range(NT):
                        last = tp(ps[jt % 2][:, cols(t)], q[:, t, cols(jt)], ident[:, :])
                    last.then_inc(setT, 1)
                pe.wait_ge(ld_const, 16 * 9)
                for k in range(KC):
                    pe.wait_ge(setT_used, NT - 1 + k)
                    for half in range(2):
                        for ot in range(KC):
                            last = tp(ps[k][:, half * O + ot * P:half * O + (ot + 1) * P],
                                      msg_w[:, ot, half * F + k * P:half * F + (k + 1) * P], ident[:, :])
                    last.then_inc(setT, 1)
                pe.wait_ge(weights_set, 1)
                place["now"], place["at"] = ("ahead",), banks(PROLOGUE, ("ahead",))
                make_hT(None, 0)
                feature_rows(None, 0)
                feature_columns(None, 0)
                spread(None, 0, 0)
                project(None, 0, 0)
                spread(None, 0, 1)
                transposes(None, 0, 0, 0)
                project(None, 0, 1)
                transposes(None, 0, 0, 1)
                attention(None, 0, 0)
                transposes(None, 0, 1, 0)
                project(None, 0, 2)
                transposes(None, 0, 1, 1)

            def iteration(i, now):
                heads, ahead, behind = ("heads" in now), ("ahead" in now), ("behind" in now)
                place["now"], place["at"] = now, banks(ITERATION, now)
                b, c = i, i - 1
                if heads:
                    out_project(0, b)
                    attention(i, b, 1)
                    spread(i, b, 2)
                    project(i, b, 3)
                if ahead:
                    make_hT(i, b + 1)
                if behind:
                    transposes(i, c, OUT, 0)
                if ahead:
                    feature_rows(i, b + 1)
                if heads:
                    spread(i, b, 3)
                if behind:
                    transposes(i, c, OUT, 1)
                    attention(i, c, OUT)
                if ahead:
                    feature_columns(i, b + 1)
                if heads:
                    transposes(i, b, 2, 0)
                    out_project(1, b)
                    transposes(i, b, 2, 1)
                if ahead:
                    spread(i, b + 1, 0)
                if heads:
                    attention(i, b, 2)
                    transposes(i, b, 3, 0)
                if behind:
                    ffn_up(i, c)
                if heads:
                    transposes(i, b, 3, 1)
                if ahead:
                    spread(i, b + 1, 1)
                if heads:
                    attention(i, b, 3)
                    out_project(2, b)
                if ahead:
                    project(i, b + 1, 0)
                    transposes(i, b + 1, 0, 0)
                if behind:
                    ffn_down(i, c)
                if ahead:
                    transposes(i, b + 1, 0, 1)
                    attention(i, b + 1, 0)
                if heads:
                    out_project(3, b)
                if ahead:
                    project(i, b + 1, 1)
                    transposes(i, b + 1, 1, 0)
                    project(i, b + 1, 2)
                    transposes(i, b + 1, 1, 1)
                if behind:
                    make_h3T(i, c)
                if heads:
                    out_features(i, b)
                if behind:
                    messages(i, c)
                if heads:
                    spread(i, b, OUT)
                if behind:
                    gather(i, c)

            program(pe, prologue, iteration)

        @block.scalar
        def _(act):
            def copy(out_ap, in_ap):
                return nc.scalar.activation(out_ap, in_ap, ACT.Copy)

            def split_hT(b):
                if later(b):
                    act.wait_ge(w_mm[1], 4 * b)
                for k in range(KC):
                    act.wait_ge(a_T, KC * b + k + 1)
                    nc.scalar.activation(hT[0][:, k, :], psum("hT", k)[:, :], ACT.Relu).then_inc(a_Th, 1)

            def feature_rows(b):
                act.wait_ge(a_f, b + 1)
                if later(b):
                    act.wait_ge(a_c, b)
                    act.wait_ge(a_fl, b)
                copy(feat[:, :], psum("featrow", 0)[0:2 * H, :]).then_inc(a_fe, 1)
                if later(b):
                    act.wait_ge(u_row, unit(3, b - 1) + 1)
                copy(featrow[0:2 * H, :], psum("featrow", 0)[0:2 * H, :]).then_inc(a_fh, 1)

            def feature_columns(b):
                act.wait_ge(a_c, b + 1)
                if later(b):
                    act.wait_ge(u_m, unit(3, b - 1) + 1)
                    act.wait_ge(a_cn, b)
                copy(f1col[:, :, :], psum("featcol", 0)[:, 0:2 * H * NT].rearrange("p (t h) -> p t h", t=NT)).then_inc(a_cc, 1)

            def row_copy(b, u):
                n = unit(u, b)
                act.wait_ge(u_row, n + 1)
                if later(n):
                    act.wait_ge(u_q, NT * n)
                copy(row[:, :], psum("rowout" if u == OUT else f"row{u}", 0)[:, :]).then_inc(u_rowc, 1)

            def values(b, h, user):
                if user is not None:
                    act.wait_ge(u_at, NT * user + NT)
                for half in range(2):
                    act.wait_ge(w_mm[h // 2], 4 * b + 2 * (h % 2) + half + 1)
                    copy(Wh[0][:, h % 2, cols(half, 2), :],
                         psum(f"proj{h}", half)[:, :].rearrange("p (t o) -> p t o", t=2)).then_inc(w_hi[h // 2], 1)

            def exps(b, u):
                n, p = unit(u, b), pp[SLOT[u]]
                act.wait_ge(u_m, n + 1)
                if later(n):
                    act.wait_ge(u_r, n)
                for t in range(NT):
                    act.wait_ge(u_l, NT * n + t + 1)
                    nc.scalar.activation(p[:, t, :], q[:, t, :], ACT.Exp, bias=nb[:, t:t + 1],
                                         accum_out=rsum[:, t:t + 1]).then_inc(u_e, 1)

            def prob_hi(b, u, half):
                n = unit(u, b)
                for jt in (2 * half, 2 * half + 1):
                    act.wait_ge(u_tr, NT * n + jt + 1)
                    if later(n):
                        act.wait_ge(u_at, NT * (n - 1) + jt + 1)
                    copy(pT[0][:, jt, :], psum(f"tr{u}", jt)[:, :]).then_inc(u_hi, 1)

            def elu_exp(b, u):
                n = unit(u, b)
                act.wait_ge(u_at, NT * n + NT)
                for ot in range(KC):
                    if later(n):
                        act.wait_ge(u_yl, KC * (n - 1) + ot + 1)
                    nc.scalar.activation(yb[:, ot, :], ps[OT[ot]][:, :], ACT.Exp).then_inc(u_E, 1)
                for ot in range(KC):
                    act.wait_ge(u_E, KC * n + ot + 1)
                    nc.scalar.activation(yb[:, ot, :], yb[:, ot, :], ACT.Copy, bias=-1.0).then_inc(u_E1, 1)

            def elu_hi(b, u, free):
                n = unit(u, b)
                if free is not None:
                    act.wait_ge(*free)
                for ot in range(KC):
                    act.wait_ge(u_y, KC * n + ot + 1)
                    copy(outputs(u)[0][:, ot, :], yb[:, ot, :]).then_inc(u_yh, 1)

            def head_free(b, h):
                count = 4 * b + h
                return (acc, count) if later(count) else None

            def out_values(c):
                act.wait_ge(acc, 4 * c + 4)
                if later(c):
                    act.wait_ge(b_2, 2 * c)
                for half in range(2):
                    copy(WM[0][:, cols(half, 2), :],
                         ps[AC[half]][:, :].rearrange("p (t o) -> p t o", t=2)).then_inc(b_Wh, 1)

            def out_rows(c):
                act.wait_ge(b_fT, c + 1)
                if later(c):
                    act.wait_ge(u_row, unit(OUT, c - 1) + 1)
                copy(forow[0:2, :], psum("featout", 0)[0:2, :]).then_inc(b_fTh, 1)

            def ffn_relu(c):
                if later(c):
                    act.wait_ge(b_T, KC * c)
                for dt in range(KC):
                    act.wait_ge(b_1, KC * c + dt + 1)
                    nc.scalar.activation(relu_y[:, dt, :], psum("ffn1", dt)[:, :], ACT.Relu,
                                         bias=b1col[:, dt:dt + 1]).then_inc(b_r, 1)

            def relu_hi(c):
                act.wait_ge(u_at, NT * unit(OUT, c) + NT)
                for dt in range(KC):
                    act.wait_ge(b_r, KC * c + dt + 1)
                    copy(r[0][:, dt, :], relu_y[:, dt, :]).then_inc(b_rh, 1)

            def ffn_out(c, half):
                act.wait_ge(b_rl, KC * c + KC)
                act.wait_ge(b_2, 2 * c + half + 1)
                copy(y[:, cols(half, 2), :], psum("ffn2", half)[:, :].rearrange("p (t o) -> p t o", t=2)).then_inc(b_y, 1)

            def split_h3T(c):
                act.wait_ge(b_2, 2 * c + 2)
                for k in range(KC):
                    act.wait_ge(b_T, KC * c + k + 1)
                    nc.scalar.activation(oh[0][:, k, :], psum("h3T", k)[:, :], ACT.Relu).then_inc(b_Th, 1)

            def message_hi(c, half):
                if half == 0 and later(c):
                    act.wait_ge(b_g, 2 * c)
                for t in (2 * half, 2 * half + 1):
                    act.wait_ge(b_l, NT * c + t + 1)
                    copy(M[0][:, t, :], psum("lin", t)[:, O:2 * O]).then_inc(b_mh, 1)

            def prologue():
                act.wait_ge(ld_const, 16 * 9)
                split_hT(0)
                act.wait_ge(ids_made, 5)
                feature_rows(0)
                feature_columns(0)
                row_copy(0, 0)
                values(0, 0, None)
                row_copy(0, 1)
                exps(0, 0)
                prob_hi(0, 0, 0)
                values(0, 1, None)
                prob_hi(0, 0, 1)
                exps(0, 1)
                elu_exp(0, 0)
                elu_hi(0, 0, None)
                prob_hi(0, 1, 0)
                values(0, 2, unit(0, 0))
                prob_hi(0, 1, 1)

            def iteration(i, now):
                heads, ahead, behind = ("heads" in now), ("ahead" in now), ("behind" in now)
                b, c = i, i - 1
                if behind:
                    exps(c, OUT)
                if heads:
                    row_copy(b, 2)
                    elu_exp(b, 1)
                    values(b, 3, unit(1, b))
                if ahead:
                    split_hT(b + 1)
                if heads:
                    elu_hi(b, 1, head_free(b, 1))
                if behind:
                    prob_hi(c, OUT, 0)
                if ahead:
                    feature_rows(b + 1)
                if heads:
                    row_copy(b, 3)
                if behind:
                    prob_hi(c, OUT, 1)
                if heads:
                    exps(b, 2)
                if ahead:
                    feature_columns(b + 1)
                if behind:
                    elu_exp(c, OUT)
                if heads:
                    prob_hi(b, 2, 0)
                if behind:
                    elu_hi(c, OUT, (b_l, NT * c) if later(c) else None)
                if heads:
                    exps(b, 3)
                    prob_hi(b, 2, 1)
                if ahead:
                    row_copy(b + 1, 0)
                if heads:
                    elu_exp(b, 2)
                    prob_hi(b, 3, 0)
                    elu_hi(b, 2, head_free(b, 2))
                if ahead:
                    exps(b + 1, 0)
                if behind:
                    ffn_relu(c)
                    relu_hi(c)
                if heads:
                    prob_hi(b, 3, 1)
                if ahead:
                    row_copy(b + 1, 1)
                if heads:
                    elu_exp(b, 3)
                if ahead:
                    values(b + 1, 0, unit(2, b))
                    exps(b + 1, 1)
                if heads:
                    elu_hi(b, 3, head_free(b, 3))
                if ahead:
                    prob_hi(b + 1, 0, 0)
                if behind:
                    ffn_out(c, 0)
                    ffn_out(c, 1)
                if ahead:
                    prob_hi(b + 1, 0, 1)
                    elu_exp(b + 1, 0)
                if heads:
                    out_values(b)
                if ahead:
                    values(b + 1, 1, unit(3, b))
                    prob_hi(b + 1, 1, 0)
                    elu_hi(b + 1, 0, head_free(b + 1, 0))
                    values(b + 1, 2, unit(0, b + 1))
                    prob_hi(b + 1, 1, 1)
                if behind:
                    split_h3T(c)
                if heads:
                    out_rows(b)
                if behind:
                    message_hi(c, 0)
                    message_hi(c, 1)
                if heads:
                    row_copy(b, OUT)

            program(act, prologue, iteration)

        @block.vector
        def _(dve):
            tt, ts, stt = nc.vector.tensor_tensor, nc.vector.tensor_scalar, nc.vector.scalar_tensor_tensor

            def statistics(k, src, b):
                if k == 0:
                    dve.wait_ge(a_x, 16 * b + 16)
                for t in range(NT):
                    last = nc.vector.bn_stats(stats[k][:, t, :], src[:, t, :])
                last.then_inc(ln_sum[k], 1)
                wait_apart(dve, ln_sum[k], b + 1)
                for t in range(NT):
                    last = nc.vector.bn_aggr(mv[k][:, t, :], stats[k][:, t, :])
                last.then_inc(ln_mv[k], 1)

            def normalise(k, to, src, b, done):
                dve.wait_ge(ln_rs[k], b + 1)
                for t in range(NT):
                    last = ts(to[:, t, :], src[:, t, :], mv[k][:, t, 0:1], rstd[k][:, t:t + 1], ALU.subtract, ALU.mult)
                last.then_inc(done, 1)

            def lo_hT(b):
                for k in range(KC):
                    dve.wait_ge(a_Th, KC * b + k + 1)
                    stt(hT[1][:, k, :], psum("hT", k)[:, :], 0.0, f32(hT[0][:, k, :]), ALU.max, ALU.subtract)\
                        .then_inc(a_Tl, 1)

            def feature_lo(b):
                dve.wait_ge(a_fe, b + 1)
                dve.wait_ge(a_fh, b + 1)
                tt(featrow[32:32 + 2 * H, :], feat[:, :], f32(featrow[0:2 * H, :]), ALU.subtract).then_inc(a_fl, 1)

            def feature_neg(b):
                dve.wait_ge(a_cc, b + 1)
                if later(b):
                    dve.wait_ge(u_w, NT * unit(3, b - 1) + NT)
                ts(f1neg[:, :, :], f1col[:, :, 0:H], -(1.0 - SLOPE), None, ALU.mult).then_inc(a_cn, 1)

            def masked(b, u):
                n = unit(u, b)
                dve.wait_ge(u_rowc, n + 1)
                for t in range(NT):
                    if later(n):
                        wait_apart(dve, u_e, NT * (n - 1) + t + 1)
                    nc.vector.tensor_tensor_reduce(out=q[:, t, :], in0=mask[:, t, :], in1=row[:, :], scale=1.0, scalar=-3e38,
                                                   op0=ALU.add, op1=ALU.max, accum_out=g[:, t:t + 1]).then_inc(u_q, 1)
                dve.wait_ge(u_q, NT * n + NT)
                f1, _ = scalars(u)
                tt(s[:, :], g[:, :], f1, ALU.add).then_inc(u_s, 1)
                dve.wait_ge(u_s, 2 * n + 1)
                stt(m[:, :], s[:, :], SLOPE, s[:, :], ALU.mult, ALU.max).then_inc(u_s, 1)
                dve.wait_ge(u_s, 2 * n + 2)
                tt(nb[:, :], f1, m[:, :], ALU.subtract).then_inc(u_m, 1)

            def leaky(b, u):
                n, p = unit(u, b), pp[SLOT[u]]
                for t in range(NT):
                    dve.wait_ge(u_w, NT * n + t + 1)
                    tt(q[:, t, :], q[:, t, :], p[:, t, :], ALU.max).then_inc(u_l, 1)

            def inverse(b, u):
                n = unit(u, b)
                dve.wait_ge(u_e, NT * n + NT)
                if later(n):
                    dve.wait_ge(u_n, NT * n)
                nc.vector.reciprocal(rinv[:, :], rsum[:, :]).then_inc(u_r, 1)

            def prob_lo(b, u, half):
                n = unit(u, b)
                for jt in (2 * half, 2 * half + 1):
                    dve.wait_ge(u_hi, NT * n + jt + 1)
                    tt(pT[1][:, jt, :], psum(f"tr{u}", jt)[:, :], f32(pT[0][:, jt, :]), ALU.subtract).then_inc(u_lo, 1)

            def elu(b, u):
                n = unit(u, b)
                for ot in range(KC):
                    dve.wait_ge(u_E1, KC * n + ot + 1)
                    stt(yb[:, ot, :], yb[:, ot, :], 0.0, ps[OT[ot]][:, :], ALU.min, ALU.max).then_inc(u_y, 1)

            def values_lo(b, h):
                for half in range(2):
                    dve.wait_ge(w_hi[h // 2], 4 * b + 2 * (h % 2) + half + 1)
                    tt(Wh[1][:, h % 2, cols(half, 2), :], psum(f"proj{h}", half)[:, :].rearrange("p (t o) -> p t o", t=2),
                       f32(Wh[0][:, h % 2, cols(half, 2), :]), ALU.subtract).then_inc(w_lo[h // 2], 1)

            def out_values_lo(c):
                for half in range(2):
                    dve.wait_ge(b_Wh, 2 * c + half + 1)
                    tt(WM[1][:, cols(half, 2), :], ps[AC[half]][:, :].rearrange("p (t o) -> p t o", t=2),
                       f32(WM[0][:, cols(half, 2), :]), ALU.subtract).then_inc(b_Wl, 1)

            def out_scalars(c, half):
                if half == 0 and later(c):
                    dve.wait_ge(b_fT, c)
                for t in (2 * half, 2 * half + 1):
                    for j in range(2):
                        k = 2 * t + j
                        if k:
                            dve.wait_ge(b_junk, 7 * c + k)
                        last = nc.vector.tensor_tensor_reduce(
                            out=junk[:, :], in0=ps[AC[t // 2]][:, cols(t % 2, O)], in1=aout[:, cols(j, O)],
                            scale=1.0, scalar=0.0, op0=ALU.mult, op1=ALU.add, accum_out=fo[:, t, j:j + 1])
                        last.then_inc(b_junk if k < 7 else b_fo, 1)
                if half == 0:
                    return
                dve.wait_ge(b_fo, c + 1)
                ts(foneg[:, :], fo[:, :, 0], -(1.0 - SLOPE), None, ALU.mult).then_inc(b_fn, 1)

            def out_rows_lo(c):
                dve.wait_ge(b_fTh, c + 1)
                tt(forow[32:34, :], psum("featout", 0)[0:2, :], f32(forow[0:2, :]), ALU.subtract).then_inc(b_fTl, 1)

            def ffn_statistics(c):
                dve.wait_ge(b_y, 2 * c + 2)
                statistics(1, y, c)

            def scale_y(c):
                dve.wait_ge(ln_mv[1], c + 1)
                for t in range(NT):
                    last = stt(y[:, t, :], y[:, t, :], mv[1][:, t, 0:1], gamma[:, :], ALU.subtract, ALU.mult)
                last.then_inc(b_z, 1)

            def new_x(c):
                dve.wait_ge(b_z, c + 1)
                dve.wait_ge(ln_rs[1], c + 1)
                dve.wait_ge(b_xb, c + 1)
                for t in range(NT):
                    last = stt(xb[:, t, :], y[:, t, :], rstd[1][:, t:t + 1], xb[:, t, :], ALU.mult, ALU.add)
                last.then_inc(b_x2, 1)
                dve.wait_ge(b_x2, c + 1)
                statistics(2, xb, c)

            def lo_h3T(c):
                for k in range(KC):
                    dve.wait_ge(b_Th, KC * c + k + 1)
                    stt(oh[1][:, k, :], psum("h3T", k)[:, :], 0.0, f32(oh[0][:, k, :]), ALU.max, ALU.subtract)\
                        .then_inc(b_Tl, 1)

            def message_lo(c, half):
                for t in (2 * half, 2 * half + 1):
                    dve.wait_ge(b_mh, NT * c + t + 1)
                    tt(M[1][:, t, :], psum("lin", t)[:, O:2 * O], f32(M[0][:, t, :]), ALU.subtract).then_inc(b_ml, 1)
                    stt(xb[:, t, :], psum("lin", t)[:, 0:O], deg[:, t:t + 1], xb[:, t, :], ALU.mult, ALU.add)\
                        .then_inc(b_mi, 1)

            def result(c, half):
                dve.wait_ge(b_g, 2 * c + half + 1)
                dve.wait_ge(b_mi, NT * c + 2 * half + 2)
                tt(xb[:, cols(half, 2), :], psum("msg", half)[:, :].rearrange("p (t o) -> p t o", t=2),
                   xb[:, cols(half, 2), :], ALU.add).then_inc(b_o, 1)

            def prologue():
                steps = [0]

                def link(ins):
                    steps[0] += 1
                    ins.then_inc(step, 1)
                    dve.wait_ge(step, steps[0])

                def split(to, src):
                    link(nc.vector.tensor_copy(to[0], src))
                    return tt(to[1], src, f32(to[0]), ALU.subtract)

                statistics(0, xa, 0)
                dve.wait_ge(ld_adj, 16)
                ints = wflat(q).bitcast(I32)
                nc.vector.tensor_copy(wflat(q), ints).then_inc(adj_float, 1)
                dve.wait_ge(adj_float, 1)
                ts(wflat(mask), wflat(q), 0.0, MASKED, ALU.is_le, ALU.mult)
                link(nc.vector.reduce_sum(deg[:, :], q[:, :, :], axis=AX.X))
                normalise(0, xa, xa, 0, a_h)
                dve.wait_ge(ld_const, 16 * 9)
                dve.wait_ge(ids_made, 5)
                link(nc.vector.tensor_copy(bias[0:2, :, :], bias_f))
                link(tt(bias[32:34, :, :], bias_f, f32(bias[0:2, :, :]), ALU.subtract))
                for jt in range(NT):
                    dve.wait_ge(setT, jt + 1)
                    split(cut(adjT, ALL, jt), ps[jt % 2][:, :]).then_inc(setT_used, 1)
                for k in range(KC):
                    dve.wait_ge(setT, NT + k + 1)
                    split(cut(WmT, ALL, k), ps[k][:, :]).then_inc(setT_used, 1)
                dve.wait_ge(ld_heads, 16 * H)
                for k in range(KC):
                    for h in range(H):
                        for j in range(2):
                            link(nc.vector.tensor_tensor_reduce(
                                out=junk[:, :], in0=heads_w[:, k, h, :], in1=avec[h // 2][:, h % 2, cols(j, O)],
                                scale=1.0, scalar=0.0, op0=ALU.mult, op1=ALU.add,
                                accum_out=wa[:, k, j * H + h:j * H + h + 1]))
                nc.vector.memset(junk[:, 0:1], 0.0).then_inc(avec_taken, 1)
                for k in range(KC):
                    link(split(cut(Wp, ALL, k), heads_w[:, k, :, :].rearrange("p h o -> p (h o)")))
                nc.vector.memset(junk[:, 1:2], 0.0).then_inc(heads_taken, 1)
                link(split(cut(Wa, ALL), wa[:, :, :]))
                dve.wait_ge(ld_ffn, 32)
                link(split(cut(F1, ALL), y[:, 0:KC, :]))
                link(split(cut(F2, ALL), y[:, KC:2 * KC, :]))
                dve.wait_ge(ld_wout, 16)
                split(cut(Wo, ALL), wout_w).then_inc(weights_set, 1)
                lo_hT(0)
                feature_lo(0)
                feature_neg(0)
                masked(0, 0)
                values_lo(0, 0)
                leaky(0, 0)
                masked(0, 1)
                inverse(0, 0)
                leaky(0, 1)
                prob_lo(0, 0, 0)
                values_lo(0, 1)
                prob_lo(0, 0, 1)
                inverse(0, 1)
                elu(0, 0)
                prob_lo(0, 1, 0)
                values_lo(0, 2)
                prob_lo(0, 1, 1)

            def iteration(i, now):
                heads, ahead, behind = ("heads" in now), ("ahead" in now), ("behind" in now)
                b, c = i, i - 1
                if behind:
                    leaky(c, OUT)
                if ahead:
                    statistics(0, xa, b + 1)
                if behind:
                    inverse(c, OUT)
                if ahead:
                    normalise(0, xa, xa, b + 1, a_h)
                if heads:
                    masked(b, 2)
                    elu(b, 1)
                    values_lo(b, 3)
                if ahead:
                    lo_hT(b + 1)
                if heads:
                    leaky(b, 2)
                if behind:
                    prob_lo(c, OUT, 0)
                if ahead:
                    feature_lo(b + 1)
                if behind:
                    prob_lo(c, OUT, 1)
                if heads:
                    masked(b, 3)
                    inverse(b, 2)
                    leaky(b, 3)
                if ahead:
                    feature_neg(b + 1)
                if behind:
                    elu(c, OUT)
                if heads:
                    prob_lo(b, 2, 0)
                    prob_lo(b, 2, 1)
                    inverse(b, 3)
                if ahead:
                    masked(b + 1, 0)
                if heads:
                    elu(b, 2)
                    prob_lo(b, 3, 0)
                if ahead:
                    leaky(b + 1, 0)
                if heads:
                    prob_lo(b, 3, 1)
                if ahead:
                    inverse(b + 1, 0)
                    masked(b + 1, 1)
                if heads:
                    elu(b, 3)
                if ahead:
                    leaky(b + 1, 1)
                    values_lo(b + 1, 0)
                    inverse(b + 1, 1)
                    prob_lo(b + 1, 0, 0)
                if behind:
                    ffn_statistics(c)
                if ahead:
                    prob_lo(b + 1, 0, 1)
                if behind:
                    scale_y(c)
                    new_x(c)
                if ahead:
                    elu(b + 1, 0)
                if behind:
                    normalise(2, y, xb, c, b_h3)
                if heads:
                    out_values_lo(b)
                if ahead:
                    values_lo(b + 1, 1)
                if heads:
                    out_scalars(b, 0)
                if ahead:
                    prob_lo(b + 1, 1, 0)
                if heads:
                    out_scalars(b, 1)
                if ahead:
                    values_lo(b + 1, 2)
                    prob_lo(b + 1, 1, 1)
                if behind:
                    lo_h3T(c)
                if heads:
                    out_rows_lo(b)
                if behind:
                    message_lo(c, 0)
                    message_lo(c, 1)
                if heads:
                    masked(b, OUT)
                if behind:
                    result(c, 0)
                    result(c, 1)

            program(dve, prologue, iteration)

        @block.gpsimd
        def _(pool):
            tt, ts = nc.gpsimd.tensor_tensor, nc.gpsimd.tensor_scalar

            def deviation(k, b):
                wait_apart(pool, ln_mv[k], b + 1)
                ts(ve[k][:, :], mv[k][:, :, 1], 1.0, EPS, ALU.mult, ALU.add).then_inc(ln_ve[k], 1)
                pool.wait_ge(ln_ve[k], b + 1)
                tt(rstd[k][:, :], ve[k][:, :], rsq[:, :], ALU.pow).then_inc(ln_rs[k], 1)

            def other_slope(b, u):
                n, was, p = unit(u, b), slot_before(u, b), pp[SLOT[u]]
                if was is not None:
                    pool.wait_ge(u_tr, NT * was + NT)
                pool.wait_ge(*((b_fn, b + 1) if u == OUT else (a_cn, b + 1)))
                _, f1n = scalars(u)
                for t in range(NT):
                    wait_apart(pool, u_q, NT * n + t + 1)
                    ts(p[:, t, :], q[:, t, :], SLOPE, f1n[:, t:t + 1], ALU.mult, ALU.add).then_inc(u_w, 1)

            def normalise_rows(b, u):
                n, p = unit(u, b), pp[SLOT[u]]
                wait_apart(pool, u_r, n + 1)
                for t in range(NT):
                    ts(p[:, t, :], p[:, t, :], rinv[:, t:t + 1], 1.0, ALU.mult, ALU.mult).then_inc(u_n, 1)

            def elu_lo(b, u):
                n, to = unit(u, b), outputs(u)
                for ot in range(KC):
                    pool.wait_ge(u_yh, KC * n + ot + 1)
                    tt(to[1][:, ot, :], yb[:, ot, :], f32(to[0][:, ot, :]), ALU.subtract).then_inc(u_yl, 1)

            def relu_lo(c):
                for dt in range(KC):
                    pool.wait_ge(b_rh, KC * c + dt + 1)
                    tt(r[1][:, dt, :], relu_y[:, dt, :], f32(r[0][:, dt, :]), ALU.subtract).then_inc(b_rl, 1)

            def add_beta(c):
                pool.wait_ge(b_x, 16 * c + 16)
                for t in range(NT):
                    last = tt(xb[:, t, :], xb[:, t, :], beta[:, :], ALU.add)
                last.then_inc(b_xb, 1)

            def prologue():
                nc.gpsimd.memset(ident[:, :], 0.0).then_inc(ids_step, 1)
                nc.gpsimd.memset(pick_f, 0.0).then_inc(ids_step, 1)
                nc.gpsimd.memset(rsq[:, :], -0.5)
                pool.wait_ge(ids_step, 2)
                nc.gpsimd.affine_select(out=ident[:, :], in_=ident[:, :], compare_op=ALU.not_equal, fill=1.0, base=0,
                                        pattern=[[-1, P]], channel_multiplier=1).then_inc(ids_made, 1)
                for k, shift in enumerate((0, 32)):
                    nc.gpsimd.affine_select(out=pick_f[:, 0, :], in_=pick_f[:, 0, :], compare_op=ALU.not_equal, fill=1.0,
                                            base=-(1 + shift), pattern=[[0, P]], channel_multiplier=1)
                    nc.gpsimd.affine_select(out=pick_f[:, 1:5, :], in_=pick_f[:, 1:5, :], compare_op=ALU.not_equal, fill=1.0,
                                            base=-(H + shift), pattern=[[-1, H], [0, P]], channel_multiplier=1).then_inc(ids_step, 1)
                    pool.wait_ge(ids_step, 3 + k)
                wait_apart(pool, ids_made, 1)
                ts(ident_r[:, :], ident[:, :], 1.0, 1.0, ALU.mult, ALU.mult).then_inc(ids_made, 1)
                ts(pick[:, :, :], pick_f, 1.0, 1.0, ALU.mult, ALU.mult).then_inc(ids_made, 1)
                nc.gpsimd.memset(featrow[:, :].bitcast(F32), 0.0).then_inc(ids_made, 1)
                nc.gpsimd.memset(bias[:, :, :].bitcast(F32), 0.0)
                nc.gpsimd.memset(forow[:, :].bitcast(F32), 0.0).then_inc(ids_made, 1)
                pool.wait_ge(ids_made, 5)
                deviation(0, 0)
                other_slope(0, 0)
                other_slope(0, 1)
                normalise_rows(0, 0)
                normalise_rows(0, 1)
                elu_lo(0, 0)

            def iteration(i, now):
                heads, ahead, behind = ("heads" in now), ("ahead" in now), ("behind" in now)
                b, c = i, i - 1
                if ahead:
                    deviation(0, b + 1)
                if behind:
                    normalise_rows(c, OUT)
                if heads:
                    other_slope(b, 2)
                    elu_lo(b, 1)
                    other_slope(b, 3)
                    normalise_rows(b, 2)
                if behind:
                    elu_lo(c, OUT)
                if heads:
                    normalise_rows(b, 3)
                if ahead:
                    other_slope(b + 1, 0)
                if heads:
                    elu_lo(b, 2)
                if behind:
                    relu_lo(c)
                if ahead:
                    normalise_rows(b + 1, 0)
                    other_slope(b + 1, 1)
                if behind:
                    add_beta(c)
                if heads:
                    elu_lo(b, 3)
                if ahead:
                    normalise_rows(b + 1, 1)
                if behind:
                    deviation(1, c)
                    deviation(2, c)
                if ahead:
                    elu_lo(b + 1, 0)
                if heads:
                    other_slope(b, OUT)

            program(pool, prologue, iteration)


_INS = ["x", "adj", "L0_gnn_W_heads", "L0_gnn_a_heads", "L0_gnn_W_out", "L0_gnn_a_out", "L0_gnn_w1", "L0_gnn_b1",
        "L0_gnn_w2", "L0_gnn_b2", "L0_gnn_ln_gamma", "L0_gnn_ln_beta", "L1_gnn_W", "L1_gnn_b"]


def kernel(**inputs):
    import numpy as _np
    import concourse.bacc as _bacc
    from concourse import mybir as _mybir
    from concourse.bass_utils import run_bass_kernel_spmd as _run

    nc = _bacc.Bacc("TRN2", target_bir_lowering=False, num_devices=1)
    arrays, args = {}, []
    for name in _INS:
        a = _np.ascontiguousarray(inputs[name])
        arrays[f"in_{name}"] = a
        args.append(nc.dram_tensor(f"in_{name}", a.shape, _mybir.dt.from_np(a.dtype), kind="ExternalInput").ap())
    shape = arrays["in_x"].shape
    args.append(nc.dram_tensor("out_0", shape, _mybir.dt.float32, kind="ExternalOutput").ap())
    gnn_kernel(nc, *args)
    got = _run(nc, [arrays], core_ids=[0])
    return got.results[0]["out_0"]
```

```python
from contextlib import ExitStack

import concourse.bass as bass
from concourse import mybir

F32 = mybir.dt.float32
F32R = mybir.dt.float32r
BF16 = mybir.dt.bfloat16
I32 = mybir.dt.int32
ALU = mybir.AluOpType
ACT = mybir.ActivationFunctionType
AX = mybir.AxisListType

P = 128
SLOPE = 0.01
EPS = 1e-5
MASKED = -float(2 ** 100)
OUT = "out"
SLOT = {1: 0, OUT: 1, 2: 2, 3: 0, 0: 1}
TR, GA, OT, AC = (0, 1), (2, 3), (4, 5), (6, 7)

PROLOGUE = [
    ("hT", 0, "ahead", 0), ("hT", 1, "ahead", 1), ("featrow", 0, "ahead", 3), ("featcol", 0, "ahead", 2),
    ("row0", 0, "ahead", 3), ("proj0", 0, "ahead", 2), ("proj0", 1, "ahead", 3), ("row1", 0, "ahead", 3),
    ("tr0", 0, "ahead", 0), ("tr0", 1, "ahead", 1), ("proj1", 0, "ahead", 2), ("proj1", 1, "ahead", 3),
    ("tr0", 2, "ahead", 0), ("tr0", 3, "ahead", 1), ("tr1", 0, "ahead", 0), ("tr1", 1, "ahead", 1),
    ("proj2", 0, "ahead", 3), ("proj2", 1, "ahead", 2), ("tr1", 2, "ahead", 0), ("tr1", 3, "ahead", 1),
]
ITERATION = [
    ("proj3", 0, "heads", 3), ("row2", 0, "heads", 2), ("proj3", 1, "heads", 2), ("hT", 0, "ahead", 0),
    ("hT", 1, "ahead", 1), ("trout", 0, "behind", 0), ("trout", 1, "behind", 1), ("featrow", 0, "ahead", 3),
    ("row3", 0, "heads", 2), ("trout", 2, "behind", 0), ("trout", 3, "behind", 1), ("featcol", 0, "ahead", 2),
    ("tr2", 0, "heads", 0), ("tr2", 1, "heads", 1), ("tr2", 2, "heads", 0), ("tr2", 3, "heads", 1),
    ("row0", 0, "ahead", 3), ("ffn1", 0, "behind", 2), ("ffn1", 1, "behind", 3), ("tr3", 0, "heads", 0),
    ("tr3", 1, "heads", 1), ("proj0", 0, "ahead", 2), ("row1", 0, "ahead", 3), ("tr3", 2, "heads", 0),
    ("tr3", 3, "heads", 1), ("ffn2", 0, "behind", 3), ("ffn2", 1, "behind", 2), ("proj0", 1, "ahead", 3),
    ("proj1", 0, "ahead", 2), ("tr0", 0, "ahead", 0), ("tr0", 1, "ahead", 1), ("proj1", 1, "ahead", 3),
    ("tr0", 2, "ahead", 0), ("tr0", 3, "ahead", 1), ("tr1", 0, "ahead", 0), ("tr1", 1, "ahead", 1),
    ("proj2", 0, "ahead", 3), ("tr1", 2, "ahead", 0), ("tr1", 3, "ahead", 1), ("proj2", 1, "ahead", 2),
    ("h3T", 0, "behind", 0), ("h3T", 1, "behind", 1), ("featout", 0, "heads", 2), ("lin", 0, "behind", 3),
    ("lin", 1, "behind", 2), ("lin", 2, "behind", 3), ("lin", 3, "behind", 2), ("rowout", 0, "heads", 3),
    ("msg", 0, "behind", 3), ("msg", 1, "behind", 2),
]
ALL_OF_IT = ("heads", "ahead", "behind")


def banks(steps, who):
    at, last = {}, {}
    for step, n, whose, bank in steps:
        if whose in who:
            at[step, n] = (bank, last.get(bank))
            last[bank] = (step, n)
    return at, last


def gnn_kernel(nc, x, adj, W_heads, a_heads, W_out, a_out, w1, b1, w2, b2, ln_gamma, ln_beta, W_msg, b_msg, out):
    NB, N, F = x.shape
    H, _, O = W_heads.shape
    NT, KC, HC = N // P, F // P, H * O // P

    def unit(u, b):
        if u == OUT:
            return 5 * NB - 1 if isinstance(b, int) and b == NB - 1 else 5 * b + 6
        if isinstance(b, int) and b == 0:
            return u
        return 5 * b + {0: -1, 1: 0, 2: 2, 3: 3}[u]

    def slot_before(u, b):
        first = isinstance(b, int) and b == 0
        if u == OUT:
            return unit(OUT, b - 1) if isinstance(b, int) and b == NB - 1 else unit(0, b + 1)
        if u == 0:
            return None if first else 0 if isinstance(b, int) and b == 1 else unit(OUT, b - 2)
        if u == 3:
            return unit(1, b)
        return None if first else unit({1: 3, 2: 2}[u], b - 1)

    ctx = ExitStack()
    with ctx:
        def sb(name, shape, dt=F32):
            return ctx.enter_context(nc.sbuf_tensor(name, shape, dt))

        def sem(name):
            return ctx.enter_context(nc.semaphore(name))

        def pair(name, shape):
            return sb(name + "_hi", shape, F32R), sb(name + "_lo", shape, F32R)

        ident = sb("ident", [P, P])
        ident_r = sb("ident_r", [P, P], F32R)
        Wp = pair("Wp", [P, KC, H * O])
        Wa = pair("Wa", [P, KC, 2 * H])
        Wo = pair("Wo", [P, HC, O])
        F1 = pair("F1", [P, KC, O])
        F2 = pair("F2", [P, KC, O])
        WmT = pair("WmT", [P, KC, 2 * O])
        adjT = pair("adjT", [P, NT, N])
        mask = sb("mask", [P, NT, N], BF16)
        deg = sb("deg", [P, NT])
        gamma = sb("gamma", [P, O])
        beta = sb("beta", [P, O])
        bias = sb("bias", [64, 2, O], F32R)
        aout = sb("aout", [P, 2 * O])
        b1col = sb("b1col", [P, KC])
        rsq = sb("rsq", [P, NT])
        pick = sb("pick", [64, 5, P], F32R)
        xa = sb("xa", [P, NT, F])
        hT = pair("hT", [P, KC, N])
        feat = sb("feat", [2 * H, N])
        featrow = sb("featrow", [64, N], F32R)
        f1col = sb("f1col", [P, NT, 2 * H])
        f1neg = sb("f1neg", [P, NT, H])
        row = sb("row", [P, N])
        q = sb("q", [P, NT, N])
        pp = [sb(f"p{k}", [P, NT, N]) for k in range(3)]
        g = sb("g", [P, NT])
        s = sb("s", [P, NT])
        m = sb("m", [P, NT])
        nb = sb("nb", [P, NT])
        rsum = sb("rsum", [P, NT])
        rinv = sb("rinv", [P, NT])
        pT = pair("pT", [P, NT, N])
        Wh = pair("Wh", [P, 2, NT, O])
        yb = sb("yb", [P, KC, N])
        h2 = pair("h2", [P, KC, N])
        xb = sb("xb", [P, NT, F])
        WM = pair("WM", [P, NT, O])
        M = pair("M", [P, NT, O])
        oh = pair("oh", [P, KC, N])
        y = sb("y", [P, NT, O])
        fo = sb("fo", [P, NT, 2])
        foneg = sb("foneg", [P, NT])
        forow = sb("forow", [64, N], F32R)
        junk = sb("junk", [P, O])
        stats = [sb(f"stats{k}", [P, NT, 6]) for k in range(3)]
        mv = [sb(f"mv{k}", [P, NT, 2]) for k in range(3)]
        ve = [sb(f"ve{k}", [P, NT]) for k in range(3)]
        rstd = [sb(f"rstd{k}", [P, NT]) for k in range(3)]
        shift = [sb(f"shift{k}", [P, NT]) for k in range(3)]
        ps = [ctx.enter_context(nc.psum_tensor(f"bank{k}", [P, 512], F32)) for k in range(8)]

        ld_adj, ld_heads, ld_avec = sem("ld_adj"), sem("ld_heads"), sem("ld_avec")
        ld_msg, ld_const, ld_late = sem("ld_msg"), sem("ld_const"), sem("ld_late")
        ids_step = sem("ids_step")
        passed = sem("passed")
        ids_made = sem("ids_made")
        step = sem("step")
        adj_float = sem("adj_float")
        setT = sem("setT")
        set_hi = sem("set_hi")
        wa_made = sem("wa_made")
        msg_set = sem("msg_set")
        wa_set, wp_set = sem("wa_set"), sem("wp_set")
        adj_set = sem("adj_set")
        late_hi, late_set = sem("late_hi"), sem("late_set")
        unit_row, unit_row_copied = sem("unit_row"), sem("unit_row_copied")
        unit_masked = sem("unit_masked")
        unit_max_step, unit_max = sem("unit_max_step"), sem("unit_max")
        unit_sloped, unit_leaky = sem("unit_sloped"), sem("unit_leaky")
        unit_exp, unit_inverse, unit_normalised = sem("unit_exp"), sem("unit_inverse"), sem("unit_normalised")
        unit_transposed, probs_hi, probs_lo = sem("unit_transposed"), sem("probs_hi"), sem("probs_lo")
        unit_attended = sem("unit_attended")
        elu_exped, elu_less_one, elu_made = sem("elu_exped"), sem("elu_less_one"), sem("elu_made")
        elu_hi_made, elu_lo_made = sem("elu_hi_made"), sem("elu_lo_made")
        ln_sum = [sem(f"ln_sum{k}") for k in range(3)]
        ln_mv = [sem(f"ln_mv{k}") for k in range(3)]
        ln_ve = [sem(f"ln_ve{k}") for k in range(3)]
        ln_rs = [sem(f"ln_rs{k}") for k in range(3)]
        ln_sh = [sem(f"ln_sh{k}") for k in range(3)]
        nodes_loaded, nodes_normalised = sem("nodes_loaded"), sem("nodes_normalised")
        hT_psum, hT_hi, hT_lo = sem("hT_psum"), sem("hT_hi"), sem("hT_lo")
        feat_psum, feat_copied, feat_hi, feat_lo = sem("feat_psum"), sem("feat_copied"), sem("feat_hi"), sem("feat_lo")
        featcol_psum, featcol_copied, f1neg_made = sem("featcol_psum"), sem("featcol_copied"), sem("f1neg_made")
        values_psum = [sem("w_mm01"), sem("w_mm23")]
        values_hi_made = [sem("w_hi01"), sem("w_hi23")]
        values_lo_made = [sem("w_lo01"), sem("w_lo23")]
        head_summed = sem("head_summed")
        residual_loaded = sem("residual_loaded")
        outval_hi, outval_lo = sem("outval_hi"), sem("outval_lo")
        product_summed, fo_made, foneg_made = sem("product_summed"), sem("fo_made"), sem("foneg_made")
        fo_psum, fo_hi, fo_lo = sem("fo_psum"), sem("fo_hi"), sem("fo_lo")
        up_psum, relu_made, relu_hi_made, relu_lo_made = sem("up_psum"), sem("relu_made"), sem("relu_hi_made"), sem("relu_lo_made")
        down_psum, ffn_copied = sem("down_psum"), sem("ffn_copied")
        beta_added, y_scaled, new_x_made = sem("beta_added"), sem("y_scaled"), sem("new_x_made")
        new_x_normalised = sem("new_x_normalised")
        h3T_psum, h3T_hi, h3T_lo = sem("h3T_psum"), sem("h3T_hi"), sem("h3T_lo")
        lin_psum, msg_hi, msg_lo, own_added = sem("lin_psum"), sem("msg_hi"), sem("msg_lo"), sem("own_added")
        sums_psum, result_made, result_stored = sem("sums_psum"), sem("result_made"), sem("result_stored")

        ALL = slice(None)

        def cols(k, w=P):
            return slice(k * w, (k + 1) * w)

        def cut(t, *ix):
            return t[0][ix], t[1][ix]

        def f32(ap):
            return ap.bitcast(F32)

        def wait_apart(eng, sem, value):
            eng.wait_ge(sem, value)
            if not isinstance(value, int):
                eng.sem_inc(passed, 1)

        def later(value):
            return not isinstance(value, int) or value > 0

        def program(eng, prologue, iteration):
            prologue()
            iteration(0, ("heads", "ahead"))
            iteration(1, ("heads", "ahead", "behind"))
            with eng.Fori(2, NB - 1) as i:
                iteration(i, ("heads", "ahead", "behind"))
            iteration(NB - 1, ("heads", "behind"))
            iteration(NB, ("behind",))

        BANK = {k: v[0] for steps in (PROLOGUE, ITERATION) for k, v in banks(steps, ALL_OF_IT)[0].items()}

        def psum(name, n):
            return ps[BANK[name, n]]

        def wflat(t):
            return t[:, :, :].rearrange("p t o -> p (t o)")

        heads_w = wflat(pp[0]).rearrange("p (k h o) -> p k h o", k=KC, h=H)
        wout_w = wflat(pp[2]).rearrange("p (k o) -> p k o", k=HC)
        avec = [wflat(pp[1])[:, cols(k, 4 * O)].rearrange("p (h o) -> p h o", h=2) for k in range(2)]
        msg_w = xb[:, :, :].rearrange("p (t k) o -> p t (k o)", t=KC)
        bias_f = junk[0:2, :], yb[0:2, :, :].rearrange("p k n -> p (k n)")[:, 3 * O:4 * O]
        r = [wflat(t).rearrange("p (k n) -> p k n", k=KC) for t in WM]
        wa = row[:, 0:KC * 2 * H].rearrange("p (k j) -> p k j", k=KC)
        relu_y = wflat(y).rearrange("p (k n) -> p k n", k=KC)
        pick_f = yb[0:64, :, :].rearrange("p k n -> p (k n)")[:, 0:5 * P].rearrange("p (s n) -> p s n", s=5)

        def outputs(u):
            return oh if u == OUT else h2

        def scalars(u):
            if u == OUT:
                return fo[:, :, 0], foneg[:, :]
            return f1col[:, :, u], f1neg[:, :, u]

        block = ctx.enter_context(nc.Block())

        @block.sync
        def _(sp):
            def prologue():
                sp.dma_start(wflat(q).bitcast(I32).rearrange("p (t n) -> p t n", t=NT),
                             adj.rearrange("(t p) j -> p t j", p=P)).then_inc(ld_adj, 16)
                sp.dma_start(xa[:, :, :], x[0].rearrange("(t p) f -> p t f", p=P)).then_inc(nodes_loaded, 16)
                for h in range(H):
                    sp.dma_start(heads_w[:, :, h, :], W_heads[h].rearrange("(k p) o -> p k o", p=P)).then_inc(ld_heads, 16)
                for k in range(2):
                    sp.dma_start(avec[k], a_heads[2 * k:2 * k + 2, :].partition_broadcast(P)).then_inc(ld_avec, 16)
                sp.dma_start(msg_w, W_msg.rearrange("(t p) n -> p t n", p=P)).then_inc(ld_msg, 16)
                sp.dma_start(aout[:, :], a_out.partition_broadcast(P)).then_inc(ld_const, 16)
                for dst, src in ((gamma[:, :], ln_gamma), (beta[:, :], ln_beta), (bias_f[0], b2), (bias_f[1], b_msg)):
                    sp.dma_start(dst, src.partition_broadcast(dst.shape[0])).then_inc(ld_const, 16)
                sp.dma_start(b1col[:, :], b1.rearrange("(k p) -> p k", p=P), allow_slow_non_contiguous=True).then_inc(ld_const, 16)
                for k, w in enumerate((w1, w2)):
                    sp.dma_start(y[:, KC * k:KC * (k + 1), :], w.rearrange("(k p) o -> p k o", p=P)).then_inc(ld_late, 16)
                sp.dma_start(wout_w, W_out.rearrange("(k p) o -> p k o", p=P)).then_inc(ld_late, 16)
                sp.wait_ge(setT, NT + KC)

            def iteration(i, now):
                if "ahead" in now:
                    sp.wait_ge(hT_psum, KC * i + KC)
                    sp.dma_start(xa[:, :, :], x[i + 1].rearrange("(t p) f -> p t f", p=P)).then_inc(nodes_loaded, 16)
                if "behind" in now:
                    c = i - 1
                    if later(c):
                        sp.wait_ge(result_made, 2 * c)
                        sp.dma_start(out[c - 1].rearrange("(t p) f -> p t f", p=P), xb[:, :, :]).then_inc(result_stored, 16)
                        sp.wait_ge(result_stored, 16 * c)
                    sp.dma_start(xb[:, :, :], x[c].rearrange("(t p) f -> p t f", p=P)).then_inc(residual_loaded, 16)

            program(sp, prologue, iteration)
            sp.wait_ge(result_made, 2 * NB)
            sp.dma_start(out[NB - 1].rearrange("(t p) f -> p t f", p=P), xb[:, :, :]).then_inc(result_stored, 16)
            sp.wait_ge(result_stored, 16 * NB)

        @block.tensor
        def _(pe):
            mm, tp = nc.tensor.matmul, nc.tensor.transpose
            place = {"at": None, "before": None}

            def read(name, n, i):
                b, c, nxt = i, (None if i is None else i - 1), (0 if i is None else i + 1)
                if name[:2] == "tr":
                    return probs_lo, NT * (unit(OUT, c) if name == "trout" else unit(int(name[2:]), b if name[2:] in "23" else nxt)) + n + 1
                if name[:3] == "row":
                    return unit_row_copied, unit(OUT, b) + 1 if name == "rowout" else unit(int(name[3:]), b if name[3:] in "23" else nxt) + 1
                if name[:4] == "proj":
                    h = int(name[4:])
                    return values_lo_made[h // 2], 4 * (nxt if h < 3 else b) + 2 * (h % 2) + n + 1
                return {"hT": (hT_lo, lambda: KC * nxt + n + 1), "featrow": (feat_hi, lambda: nxt + 1), "featcol": (featcol_copied, lambda: nxt + 1),
                        "featout": (fo_lo, lambda: b + 1), "ffn1": (relu_made, lambda: KC * c + n + 1),
                        "ffn2": (ffn_copied, lambda: 2 * c + n + 1), "h3T": (h3T_lo, lambda: KC * c + n + 1),
                        "lin": (own_added, lambda: NT * c + n + 1), "msg": (result_made, lambda: 2 * c + n + 1)}[name]

            def bank(i, name, n):
                k, last = place["at"][name, n]
                if last is not None:
                    done, value = read(*last, i)
                    pe.wait_ge(done, value() if callable(value) else value)
                elif i is None:
                    if k in GA:
                        pe.wait_ge(msg_set, KC)
                else:
                    before = i == 0 if isinstance(i, int) else False
                    done, value = read(*place["before"][k], None if before else i - 1)
                    pe.wait_ge(done, value() if callable(value) else value)
                return ps[k]

            def split3(to, lhs, rhs, first, last):
                mm(to, lhs[0], rhs[0], start=first, stop=False, skip_group_check=True)
                mm(to, lhs[0], rhs[1], start=False, stop=False, skip_group_check=True)
                return mm(to, lhs[1], rhs[0], start=False, stop=last, skip_group_check=True)

            def make_hT(i, b):
                pe.wait_ge(nodes_normalised, b + 1)
                for k in range(KC):
                    to = bank(i, "hT", k)
                    for t in range(NT):
                        last = tp(to[:, cols(t)], xa[:, t, cols(k)], ident[:, :])
                    last.then_inc(hT_psum, 1)

            def feature_rows(i, b):
                to = bank(i, "featrow", 0)
                for k in range(KC):
                    pe.wait_ge(hT_lo, KC * b + k + 1)
                    last = split3(to[0:2 * H, :], cut(Wa, ALL, k), cut(hT, ALL, k), k == 0, k == KC - 1)
                last.then_inc(feat_psum, 1)

            def feature_columns(i, b):
                to = bank(i, "featcol", 0)
                wait_apart(pe, feat_copied, b + 1)
                for t in range(NT):
                    last = tp(to[:, cols(t, 2 * H)], feat[:, cols(t)], ident[0:2 * H, 0:2 * H])
                last.then_inc(featcol_psum, 1)

            def spread(i, b, u):
                if u == OUT:
                    pe.wait_ge(fo_lo, b + 1)
                    pe.wait_ge(fo_hi, b + 1)
                    to = bank(i, "rowout", 0)
                    mm(to[:, :], pick[:, 0, :], forow[:, :], start=True, stop=True).then_inc(unit_row, 1)
                else:
                    pe.wait_ge(feat_lo, b + 1)
                    pe.wait_ge(feat_hi, b + 1)
                    to = bank(i, f"row{u}", 0)
                    mm(to[:, :], pick[:, 1 + u, :], featrow[:, :], start=True, stop=True).then_inc(unit_row, 1)

            def project(i, b, h, half):
                to = bank(i, f"proj{h}", half)
                for tt in range(2):
                    for k in range(KC):
                        last = split3(to[:, cols(tt, O)], cut(hT, ALL, k, cols(2 * half + tt)),
                                      cut(Wp, ALL, k, cols(h, O)), k == 0 and tt == 0, k == KC - 1)
                last.then_inc(values_psum[h // 2], 1)

            def transposes(i, b, u, half):
                n, p = unit(u, b), pp[SLOT[u]]
                for jt in (2 * half, 2 * half + 1):
                    to = bank(i, f"tr{u}", jt)
                    for t in range(NT):
                        if jt == 0:
                            pe.wait_ge(unit_normalised, NT * n + t + 1)
                        last = tp(to[:, cols(t)], p[:, t, cols(jt)], ident[:, :])
                    last.then_inc(unit_transposed, 1)

            def attention(i, b, u):
                n = unit(u, b)
                for jt in range(NT):
                    if jt % 2 == 0 and u == OUT:
                        pe.wait_ge(outval_lo, 2 * b + jt // 2 + 1)
                    elif jt % 2 == 0:
                        pe.wait_ge(values_lo_made[u // 2], 4 * b + 2 * (u % 2) + jt // 2 + 1)
                    pe.wait_ge(probs_lo, NT * n + jt + 1)
                    for ot in range(KC):
                        if jt == 0 and later(n):
                            pe.wait_ge(elu_made, KC * (n - 1) + ot + 1)
                        val = cut(WM, ALL, jt, cols(ot)) if u == OUT else cut(Wh, ALL, u % 2, jt, cols(ot))
                        last = split3(ps[OT[ot]][:, :], val, cut(pT, ALL, jt), jt == 0, jt == NT - 1)
                    last.then_inc(unit_attended, 1)

            def out_project(h, b):
                for half in range(2):
                    if h == 0 and later(b):
                        pe.wait_ge(fo_made, b)
                    for tt in range(2):
                        for k in range(KC):
                            if half == 0 and tt == 0:
                                pe.wait_ge(elu_lo_made, KC * unit(h, b) + k + 1)
                            last = split3(ps[AC[half]][:, cols(tt, O)], cut(h2, ALL, k, cols(2 * half + tt)),
                                          cut(Wo, ALL, KC * h + k), h == 0 and k == 0 and tt == 0,
                                          h == H - 1 and k == KC - 1)
                last.then_inc(head_summed, 1)

            def out_features(i, c):
                pe.wait_ge(fo_made, c + 1)
                to = bank(i, "featout", 0)
                for t in range(NT):
                    last = tp(to[0:2, cols(t)], fo[:, t, :], ident[:, :])
                last.then_inc(fo_psum, 1)

            def ffn_up(i, c, dt):
                to = bank(i, "ffn1", dt)
                for k in range(KC):
                    if dt == 0:
                        pe.wait_ge(elu_lo_made, KC * unit(OUT, c) + k + 1)
                    last = split3(to[:, :], cut(F1, ALL, k, cols(dt)), cut(oh, ALL, k), k == 0, k == KC - 1)
                last.then_inc(up_psum, 1)

            def ffn_down(i, c, half):
                to = bank(i, "ffn2", half)
                for tt in range(2):
                    t = 2 * half + tt
                    for k in range(KC):
                        if half == 0 and tt == 0:
                            pe.wait_ge(relu_lo_made, KC * c + k + 1)
                        split3(to[:, cols(tt, O)], cut(r, ALL, k, cols(t)), cut(F2, ALL, k), k == 0 and tt == 0, False)
                    for k in range(KC):
                        for part in oh:
                            mm(to[:, tt * O + k * P:tt * O + (k + 1) * P], part[:, k, cols(t)], ident_r[:, :],
                               start=False, stop=False, skip_group_check=True)
                    last = mm(to[:, cols(tt, O)], pick[:, 0, :], bias[:, 0, :], start=False, stop=True, skip_group_check=True)
                last.then_inc(down_psum, 1)

            def make_h3T(i, c):
                pe.wait_ge(new_x_normalised, c + 1)
                for k in range(KC):
                    to = bank(i, "h3T", k)
                    for t in range(NT):
                        last = tp(to[:, cols(t)], y[:, t, cols(k)], ident[:, :])
                    last.then_inc(h3T_psum, 1)

            def messages(i, c, half):
                for t in (2 * half, 2 * half + 1):
                    to = bank(i, "lin", t)
                    for k in range(KC):
                        if t == 0:
                            pe.wait_ge(h3T_lo, KC * c + k + 1)
                        split3(to[:, :], cut(oh, ALL, k, cols(t)), cut(WmT, ALL, k), k == 0, False)
                    mm(to[:, 0:O], pick[:, 0, :], bias[:, 1, :], start=False, stop=True, skip_group_check=True).then_inc(lin_psum, 1)

            def gather(i, c, half):
                to = bank(i, "msg", half)
                for tt in range(2):
                    for jt in range(NT):
                        if half == 0 and tt == 0:
                            pe.wait_ge(msg_lo, NT * c + jt + 1)
                        last = split3(to[:, cols(tt, O)], cut(adjT, ALL, jt, cols(2 * half + tt)), cut(M, ALL, jt),
                                      jt == 0 and tt == 0, jt == NT - 1)
                last.then_inc(sums_psum, 1)

            def prologue():
                pe.wait_ge(ids_made, 3)
                pe.wait_ge(adj_float, 1)
                for jt in range(NT):
                    for t in range(NT):
                        last = tp(ps[(OT + AC)[jt]][:, cols(t)], q[:, t, cols(jt)], ident[:, :])
                    last.then_inc(setT, 1)
                pe.wait_ge(ld_msg, 16)
                for k in range(KC):
                    for half in range(2):
                        for ot in range(KC):
                            last = tp(ps[GA[k]][:, half * O + ot * P:half * O + (ot + 1) * P],
                                      msg_w[:, ot, half * F + k * P:half * F + (k + 1) * P], ident[:, :])
                    last.then_inc(setT, 1)
                place["at"], place["before"] = banks(PROLOGUE, ("ahead",))
                make_hT(None, 0)
                pe.wait_ge(wa_set, 1)
                feature_rows(None, 0)
                feature_columns(None, 0)
                spread(None, 0, 0)
                pe.wait_ge(wp_set, KC)
                project(None, 0, 0, 0)
                project(None, 0, 0, 1)
                spread(None, 0, 1)
                transposes(None, 0, 0, 0)
                project(None, 0, 1, 0)
                project(None, 0, 1, 1)
                transposes(None, 0, 0, 1)
                pe.wait_ge(adj_set, NT)
                attention(None, 0, 0)
                transposes(None, 0, 1, 0)
                project(None, 0, 2, 0)
                project(None, 0, 2, 1)
                transposes(None, 0, 1, 1)
                pe.wait_ge(late_set, 3)

            def iteration(i, now):
                heads, ahead, behind = ("heads" in now), ("ahead" in now), ("behind" in now)
                place["at"], last = banks(ITERATION, now)
                b, c = i, i - 1
                if heads:
                    project(i, b, 3, 0)
                    spread(i, b, 2)
                    attention(i, b, 1)
                    project(i, b, 3, 1)
                if ahead:
                    make_hT(i, b + 1)
                if heads:
                    out_project(0, b)
                if behind:
                    transposes(i, c, OUT, 0)
                if ahead:
                    feature_rows(i, b + 1)
                if heads:
                    spread(i, b, 3)
                if behind:
                    transposes(i, c, OUT, 1)
                    attention(i, c, OUT)
                if ahead:
                    feature_columns(i, b + 1)
                if heads:
                    transposes(i, b, 2, 0)
                    out_project(1, b)
                    transposes(i, b, 2, 1)
                if ahead:
                    spread(i, b + 1, 0)
                if heads:
                    attention(i, b, 2)
                if behind:
                    ffn_up(i, c, 0)
                    ffn_up(i, c, 1)
                if heads:
                    transposes(i, b, 3, 0)
                if ahead:
                    project(i, b + 1, 0, 0)
                    spread(i, b + 1, 1)
                if heads:
                    transposes(i, b, 3, 1)
                    attention(i, b, 3)
                if behind:
                    ffn_down(i, c, 0)
                    ffn_down(i, c, 1)
                if ahead:
                    project(i, b + 1, 0, 1)
                if heads:
                    out_project(2, b)
                if ahead:
                    project(i, b + 1, 1, 0)
                    transposes(i, b + 1, 0, 0)
                    project(i, b + 1, 1, 1)
                if heads:
                    out_project(3, b)
                if ahead:
                    transposes(i, b + 1, 0, 1)
                    attention(i, b + 1, 0)
                    transposes(i, b + 1, 1, 0)
                    project(i, b + 1, 2, 0)
                    transposes(i, b + 1, 1, 1)
                    project(i, b + 1, 2, 1)
                if behind:
                    make_h3T(i, c)
                if heads:
                    out_features(i, b)
                if behind:
                    messages(i, c, 0)
                    messages(i, c, 1)
                if heads:
                    spread(i, b, OUT)
                if behind:
                    gather(i, c, 0)
                    gather(i, c, 1)
                place["before"] = last

            program(pe, prologue, iteration)

        @block.scalar
        def _(act):
            def copy(out_ap, in_ap):
                return nc.scalar.activation(out_ap, in_ap, ACT.Copy)

            def normalise(k, to, src, b, done):
                act.wait_ge(ln_sh[k], b + 1)
                for t in range(NT):
                    last = nc.scalar.activation(to[:, t, :], src[:, t, :], ACT.Identity, bias=shift[k][:, t:t + 1],
                                                scale=rstd[k][:, t:t + 1])
                last.then_inc(done, 1)

            def split_hT(b):
                if later(b):
                    act.wait_ge(values_psum[1], 4 * b)
                for k in range(KC):
                    act.wait_ge(hT_psum, KC * b + k + 1)
                    nc.scalar.activation(hT[0][:, k, :], psum("hT", k)[:, :], ACT.Relu).then_inc(hT_hi, 1)

            def feature_rows(b):
                act.wait_ge(feat_psum, b + 1)
                if later(b):
                    act.wait_ge(featcol_psum, b)
                    act.wait_ge(feat_lo, b)
                copy(feat[:, :], psum("featrow", 0)[0:2 * H, :]).then_inc(feat_copied, 1)
                if later(b):
                    act.wait_ge(unit_row, unit(3, b - 1) + 1)
                copy(featrow[0:2 * H, :], psum("featrow", 0)[0:2 * H, :]).then_inc(feat_hi, 1)

            def feature_columns(b):
                act.wait_ge(featcol_psum, b + 1)
                if later(b):
                    act.wait_ge(unit_max, unit(3, b - 1) + 1)
                    act.wait_ge(f1neg_made, b)
                copy(f1col[:, :, :], psum("featcol", 0)[:, 0:2 * H * NT].rearrange("p (t h) -> p t h", t=NT)).then_inc(featcol_copied, 1)

            def row_copy(b, u):
                n = unit(u, b)
                act.wait_ge(unit_row, n + 1)
                if later(n):
                    act.wait_ge(unit_masked, NT * n)
                copy(row[:, :], psum("rowout" if u == OUT else f"row{u}", 0)[:, :]).then_inc(unit_row_copied, 1)

            def values(b, h, half, user):
                if user is not None:
                    act.wait_ge(unit_attended, NT * user + NT)
                act.wait_ge(values_psum[h // 2], 4 * b + 2 * (h % 2) + half + 1)
                copy(Wh[0][:, h % 2, cols(half, 2), :],
                     psum(f"proj{h}", half)[:, :].rearrange("p (t o) -> p t o", t=2)).then_inc(values_hi_made[h // 2], 1)

            def exps(b, u, half):
                n, p = unit(u, b), pp[SLOT[u]]
                if half == 0:
                    act.wait_ge(unit_max, n + 1)
                    if later(n):
                        act.wait_ge(unit_inverse, n)
                for t in (2 * half, 2 * half + 1):
                    act.wait_ge(unit_leaky, NT * n + t + 1)
                    nc.scalar.activation(p[:, t, :], q[:, t, :], ACT.Exp, bias=nb[:, t:t + 1],
                                         accum_out=rsum[:, t:t + 1]).then_inc(unit_exp, 1)

            def prob_hi(b, u, half):
                n = unit(u, b)
                for jt in (2 * half, 2 * half + 1):
                    act.wait_ge(unit_transposed, NT * n + jt + 1)
                    if later(n):
                        act.wait_ge(unit_attended, NT * (n - 1) + jt + 1)
                    copy(pT[0][:, jt, :], psum(f"tr{u}", jt)[:, :]).then_inc(probs_hi, 1)

            def elu_exp(b, u, part):
                n = unit(u, b)
                if part == 0:
                    act.wait_ge(unit_attended, NT * n + NT)
                for ot in range(KC):
                    if part == 0:
                        if later(n):
                            act.wait_ge(elu_lo_made, KC * (n - 1) + ot + 1)
                        nc.scalar.activation(yb[:, ot, :], ps[OT[ot]][:, :], ACT.Exp).then_inc(elu_exped, 1)
                    else:
                        act.wait_ge(elu_exped, KC * n + ot + 1)
                        nc.scalar.activation(yb[:, ot, :], yb[:, ot, :], ACT.Copy, bias=-1.0).then_inc(elu_less_one, 1)

            def elu_hi(b, u, free):
                n = unit(u, b)
                if free is not None:
                    act.wait_ge(*free)
                for ot in range(KC):
                    act.wait_ge(elu_made, KC * n + ot + 1)
                    copy(outputs(u)[0][:, ot, :], yb[:, ot, :]).then_inc(elu_hi_made, 1)

            def head_free(b, h):
                count = 4 * b + h
                return (head_summed, count) if later(count) else None

            def out_values(c):
                act.wait_ge(head_summed, 4 * c + 4)
                if later(c):
                    act.wait_ge(down_psum, 2 * c)
                for half in range(2):
                    copy(WM[0][:, cols(half, 2), :],
                         ps[AC[half]][:, :].rearrange("p (t o) -> p t o", t=2)).then_inc(outval_hi, 1)

            def out_rows(c):
                act.wait_ge(fo_psum, c + 1)
                if later(c):
                    act.wait_ge(unit_row, unit(OUT, c - 1) + 1)
                copy(forow[0:2, :], psum("featout", 0)[0:2, :]).then_inc(fo_hi, 1)

            def ffn_relu(c):
                if later(c):
                    act.wait_ge(h3T_psum, KC * c)
                for dt in range(KC):
                    act.wait_ge(up_psum, KC * c + dt + 1)
                    nc.scalar.activation(relu_y[:, dt, :], psum("ffn1", dt)[:, :], ACT.Relu,
                                         bias=b1col[:, dt:dt + 1]).then_inc(relu_made, 1)

            def relu_hi(c):
                act.wait_ge(unit_attended, NT * unit(OUT, c) + NT)
                for dt in range(KC):
                    act.wait_ge(relu_made, KC * c + dt + 1)
                    copy(r[0][:, dt, :], relu_y[:, dt, :]).then_inc(relu_hi_made, 1)

            def ffn_out(c, half):
                act.wait_ge(relu_lo_made, KC * c + KC)
                act.wait_ge(down_psum, 2 * c + half + 1)
                copy(y[:, cols(half, 2), :], psum("ffn2", half)[:, :].rearrange("p (t o) -> p t o", t=2)).then_inc(ffn_copied, 1)

            def split_h3T(c):
                act.wait_ge(down_psum, 2 * c + 2)
                for k in range(KC):
                    act.wait_ge(h3T_psum, KC * c + k + 1)
                    nc.scalar.activation(oh[0][:, k, :], psum("h3T", k)[:, :], ACT.Relu).then_inc(h3T_hi, 1)

            def message_hi(c, half):
                if half == 0 and later(c):
                    act.wait_ge(sums_psum, 2 * c)
                for t in (2 * half, 2 * half + 1):
                    act.wait_ge(lin_psum, NT * c + t + 1)
                    copy(M[0][:, t, :], psum("lin", t)[:, O:2 * O]).then_inc(msg_hi, 1)

            def prologue():
                normalise(0, xa, xa, 0, nodes_normalised)
                for k in range(KC):
                    act.wait_ge(setT, NT + k + 1)
                    copy(WmT[0][:, k, :], ps[GA[k]][:, :]).then_inc(set_hi, 1)
                split_hT(0)
                act.wait_ge(ld_heads, 16 * H)
                for k in range(KC):
                    copy(Wp[0][:, k, :], heads_w[:, k, :, :].rearrange("p h o -> p (h o)")).then_inc(set_hi, 1)
                for jt in range(NT):
                    act.wait_ge(setT, jt + 1)
                    copy(adjT[0][:, jt, :], ps[(OT + AC)[jt]][:, :]).then_inc(set_hi, 1)
                act.wait_ge(ld_const, 16 * 6)
                act.wait_ge(ids_made, 5)
                feature_rows(0)
                feature_columns(0)
                row_copy(0, 0)
                values(0, 0, 0, None)
                values(0, 0, 1, None)
                row_copy(0, 1)
                exps(0, 0, 0)
                exps(0, 0, 1)
                prob_hi(0, 0, 0)
                values(0, 1, 0, None)
                values(0, 1, 1, None)
                prob_hi(0, 0, 1)
                exps(0, 1, 0)
                exps(0, 1, 1)
                elu_exp(0, 0, 0)
                elu_exp(0, 0, 1)
                elu_hi(0, 0, None)
                prob_hi(0, 1, 0)
                values(0, 2, 0, unit(0, 0))
                values(0, 2, 1, unit(0, 0))
                prob_hi(0, 1, 1)

            def iteration(i, now):
                heads, ahead, behind = ("heads" in now), ("ahead" in now), ("behind" in now)
                b, c = i, i - 1
                if heads:
                    row_copy(b, 2)
                if behind:
                    exps(c, OUT, 0)
                    exps(c, OUT, 1)
                if ahead:
                    normalise(0, xa, xa, b + 1, nodes_normalised)
                if heads:
                    values(b, 3, 0, unit(1, b))
                    elu_exp(b, 1, 0)
                if ahead:
                    split_hT(b + 1)
                if heads:
                    elu_exp(b, 1, 1)
                    values(b, 3, 1, unit(1, b))
                    elu_hi(b, 1, head_free(b, 1))
                if behind:
                    prob_hi(c, OUT, 0)
                if heads:
                    exps(b, 2, 0)
                if behind:
                    prob_hi(c, OUT, 1)
                if heads:
                    exps(b, 2, 1)
                    row_copy(b, 3)
                if ahead:
                    feature_rows(b + 1)
                if behind:
                    elu_exp(c, OUT, 0)
                if heads:
                    prob_hi(b, 2, 0)
                if behind:
                    elu_exp(c, OUT, 1)
                if ahead:
                    feature_columns(b + 1)
                if heads:
                    exps(b, 3, 0)
                    prob_hi(b, 2, 1)
                if behind:
                    elu_hi(c, OUT, (lin_psum, NT * c) if later(c) else None)
                if ahead:
                    row_copy(b + 1, 0)
                if heads:
                    exps(b, 3, 1)
                    elu_exp(b, 2, 0)
                    elu_exp(b, 2, 1)
                if behind:
                    ffn_relu(c)
                if heads:
                    prob_hi(b, 3, 0)
                    elu_hi(b, 2, head_free(b, 2))
                if behind:
                    relu_hi(c)
                if heads:
                    prob_hi(b, 3, 1)
                if ahead:
                    row_copy(b + 1, 1)
                    values(b + 1, 0, 0, unit(2, b))
                    exps(b + 1, 0, 0)
                    exps(b + 1, 0, 1)
                if heads:
                    elu_exp(b, 3, 0)
                    elu_exp(b, 3, 1)
                if behind:
                    ffn_out(c, 0)
                    ffn_out(c, 1)
                if ahead:
                    exps(b + 1, 1, 0)
                    values(b + 1, 0, 1, unit(2, b))
                if heads:
                    elu_hi(b, 3, head_free(b, 3))
                if ahead:
                    prob_hi(b + 1, 0, 0)
                    values(b + 1, 1, 0, unit(3, b))
                    exps(b + 1, 1, 1)
                    values(b + 1, 1, 1, unit(3, b))
                if heads:
                    out_values(b)
                if ahead:
                    prob_hi(b + 1, 0, 1)
                if behind:
                    normalise(2, y, xb, c, new_x_normalised)
                if ahead:
                    prob_hi(b + 1, 1, 0)
                    elu_exp(b + 1, 0, 0)
                    values(b + 1, 2, 0, unit(0, b + 1))
                    prob_hi(b + 1, 1, 1)
                    values(b + 1, 2, 1, unit(0, b + 1))
                if behind:
                    split_h3T(c)
                if heads:
                    out_rows(b)
                if behind:
                    message_hi(c, 0)
                if ahead:
                    elu_exp(b + 1, 0, 1)
                if behind:
                    message_hi(c, 1)
                if heads:
                    row_copy(b, OUT)
                if ahead:
                    elu_hi(b + 1, 0, head_free(b + 1, 0))

            program(act, prologue, iteration)

        @block.vector
        def _(dve):
            tt, ts, stt = nc.vector.tensor_tensor, nc.vector.tensor_scalar, nc.vector.scalar_tensor_tensor

            def statistics(k, src, b):
                if k == 0:
                    dve.wait_ge(nodes_loaded, 16 * b + 16)
                for t in range(NT):
                    last = nc.vector.bn_stats(stats[k][:, t, :], src[:, t, :])
                last.then_inc(ln_sum[k], 1)
                wait_apart(dve, ln_sum[k], b + 1)
                for t in range(NT):
                    last = nc.vector.bn_aggr(mv[k][:, t, :], stats[k][:, t, :])
                last.then_inc(ln_mv[k], 1)

            def shifts(k, b):
                dve.wait_ge(ln_rs[k], b + 1)
                stt(shift[k][:, :], mv[k][:, :, 0], -1.0, rstd[k][:, :], ALU.mult, ALU.mult).then_inc(ln_sh[k], 1)

            def lo_hT(b):
                for k in range(KC):
                    dve.wait_ge(hT_hi, KC * b + k + 1)
                    stt(hT[1][:, k, :], psum("hT", k)[:, :], 0.0, f32(hT[0][:, k, :]), ALU.max, ALU.subtract)\
                        .then_inc(hT_lo, 1)

            def feature_lo(b):
                dve.wait_ge(feat_copied, b + 1)
                dve.wait_ge(feat_hi, b + 1)
                tt(featrow[32:32 + 2 * H, :], feat[:, :], f32(featrow[0:2 * H, :]), ALU.subtract).then_inc(feat_lo, 1)

            def feature_neg(b):
                dve.wait_ge(featcol_copied, b + 1)
                if later(b):
                    dve.wait_ge(unit_sloped, NT * unit(3, b - 1) + NT)
                ts(f1neg[:, :, :], f1col[:, :, 0:H], -(1.0 - SLOPE), None, ALU.mult).then_inc(f1neg_made, 1)

            def masked(b, u, half):
                n = unit(u, b)
                if half == 0:
                    dve.wait_ge(unit_row_copied, n + 1)
                for t in (2 * half, 2 * half + 1):
                    if later(n):
                        wait_apart(dve, unit_exp, NT * (n - 1) + t + 1)
                    nc.vector.tensor_tensor_reduce(out=q[:, t, :], in0=mask[:, t, :], in1=row[:, :], scale=1.0, scalar=-3e38,
                                                   op0=ALU.add, op1=ALU.max, accum_out=g[:, t:t + 1]).then_inc(unit_masked, 1)
                if half == 0:
                    return
                dve.wait_ge(unit_masked, NT * n + NT)
                f1, _ = scalars(u)
                tt(s[:, :], g[:, :], f1, ALU.add).then_inc(unit_max_step, 1)
                dve.wait_ge(unit_max_step, 2 * n + 1)
                stt(m[:, :], s[:, :], SLOPE, s[:, :], ALU.mult, ALU.max).then_inc(unit_max_step, 1)
                dve.wait_ge(unit_max_step, 2 * n + 2)
                tt(nb[:, :], f1, m[:, :], ALU.subtract).then_inc(unit_max, 1)

            def leaky(b, u, half):
                n, p = unit(u, b), pp[SLOT[u]]
                for t in (2 * half, 2 * half + 1):
                    dve.wait_ge(unit_sloped, NT * n + t + 1)
                    tt(q[:, t, :], q[:, t, :], p[:, t, :], ALU.max).then_inc(unit_leaky, 1)

            def inverse(b, u):
                n = unit(u, b)
                dve.wait_ge(unit_exp, NT * n + NT)
                if later(n):
                    dve.wait_ge(unit_normalised, NT * n)
                nc.vector.reciprocal(rinv[:, :], rsum[:, :]).then_inc(unit_inverse, 1)

            def prob_lo(b, u, half):
                n = unit(u, b)
                for jt in (2 * half, 2 * half + 1):
                    dve.wait_ge(probs_hi, NT * n + jt + 1)
                    tt(pT[1][:, jt, :], psum(f"tr{u}", jt)[:, :], f32(pT[0][:, jt, :]), ALU.subtract).then_inc(probs_lo, 1)

            def elu(b, u):
                n = unit(u, b)
                for ot in range(KC):
                    dve.wait_ge(elu_less_one, KC * n + ot + 1)
                    stt(yb[:, ot, :], yb[:, ot, :], 0.0, ps[OT[ot]][:, :], ALU.min, ALU.max).then_inc(elu_made, 1)

            def values_lo(b, h, half):
                dve.wait_ge(values_hi_made[h // 2], 4 * b + 2 * (h % 2) + half + 1)
                tt(Wh[1][:, h % 2, cols(half, 2), :], psum(f"proj{h}", half)[:, :].rearrange("p (t o) -> p t o", t=2),
                   f32(Wh[0][:, h % 2, cols(half, 2), :]), ALU.subtract).then_inc(values_lo_made[h // 2], 1)

            def out_values_lo(c):
                for half in range(2):
                    dve.wait_ge(outval_hi, 2 * c + half + 1)
                    tt(WM[1][:, cols(half, 2), :], ps[AC[half]][:, :].rearrange("p (t o) -> p t o", t=2),
                       f32(WM[0][:, cols(half, 2), :]), ALU.subtract).then_inc(outval_lo, 1)

            def out_scalars(c, half):
                if half == 0 and later(c):
                    dve.wait_ge(fo_psum, c)
                for t in (2 * half, 2 * half + 1):
                    for j in range(2):
                        k = 2 * t + j
                        if k:
                            dve.wait_ge(product_summed, 7 * c + k)
                        last = nc.vector.tensor_tensor_reduce(
                            out=junk[:, :], in0=ps[AC[t // 2]][:, cols(t % 2, O)], in1=aout[:, cols(j, O)],
                            scale=1.0, scalar=0.0, op0=ALU.mult, op1=ALU.add, accum_out=fo[:, t, j:j + 1])
                        last.then_inc(product_summed if k < 7 else fo_made, 1)
                if half == 0:
                    return
                dve.wait_ge(fo_made, c + 1)
                ts(foneg[:, :], fo[:, :, 0], -(1.0 - SLOPE), None, ALU.mult).then_inc(foneg_made, 1)

            def out_rows_lo(c):
                dve.wait_ge(fo_hi, c + 1)
                tt(forow[32:34, :], psum("featout", 0)[0:2, :], f32(forow[0:2, :]), ALU.subtract).then_inc(fo_lo, 1)

            def ffn_statistics(c):
                dve.wait_ge(ffn_copied, 2 * c + 2)
                statistics(1, y, c)

            def scale_y(c):
                dve.wait_ge(ln_mv[1], c + 1)
                for t in range(NT):
                    last = stt(y[:, t, :], y[:, t, :], mv[1][:, t, 0:1], gamma[:, :], ALU.subtract, ALU.mult)
                last.then_inc(y_scaled, 1)

            def new_x(c):
                dve.wait_ge(y_scaled, c + 1)
                dve.wait_ge(ln_rs[1], c + 1)
                dve.wait_ge(beta_added, c + 1)
                for t in range(NT):
                    last = stt(xb[:, t, :], y[:, t, :], rstd[1][:, t:t + 1], xb[:, t, :], ALU.mult, ALU.add)
                last.then_inc(new_x_made, 1)
                dve.wait_ge(new_x_made, c + 1)
                statistics(2, xb, c)

            def lo_h3T(c):
                for k in range(KC):
                    dve.wait_ge(h3T_hi, KC * c + k + 1)
                    stt(oh[1][:, k, :], psum("h3T", k)[:, :], 0.0, f32(oh[0][:, k, :]), ALU.max, ALU.subtract)\
                        .then_inc(h3T_lo, 1)

            def message_lo(c, half):
                for t in (2 * half, 2 * half + 1):
                    dve.wait_ge(msg_hi, NT * c + t + 1)
                    tt(M[1][:, t, :], psum("lin", t)[:, O:2 * O], f32(M[0][:, t, :]), ALU.subtract).then_inc(msg_lo, 1)
                    stt(xb[:, t, :], psum("lin", t)[:, 0:O], deg[:, t:t + 1], xb[:, t, :], ALU.mult, ALU.add)\
                        .then_inc(own_added, 1)

            def result(c, half):
                dve.wait_ge(sums_psum, 2 * c + half + 1)
                dve.wait_ge(own_added, NT * c + 2 * half + 2)
                tt(xb[:, cols(half, 2), :], psum("msg", half)[:, :].rearrange("p (t o) -> p t o", t=2),
                   xb[:, cols(half, 2), :], ALU.add).then_inc(result_made, 1)

            def prologue():
                steps = [0]

                def link(ins):
                    steps[0] += 1
                    ins.then_inc(step, 1)
                    dve.wait_ge(step, steps[0])

                statistics(0, xa, 0)
                dve.wait_ge(ld_adj, 16)
                ints = wflat(q).bitcast(I32)
                nc.vector.tensor_copy(wflat(q), ints).then_inc(adj_float, 1)
                dve.wait_ge(adj_float, 1)
                ts(wflat(mask), wflat(q), 0.0, MASKED, ALU.is_le, ALU.mult)
                link(nc.vector.reduce_sum(deg[:, :], q[:, :, :], axis=AX.X))
                shifts(0, 0)
                for k in range(KC):
                    dve.wait_ge(set_hi, k + 1)
                    tt(WmT[1][:, k, :], ps[GA[k]][:, :], f32(WmT[0][:, k, :]), ALU.subtract).then_inc(msg_set, 1)
                dve.wait_ge(ld_heads, 16 * H)
                dve.wait_ge(ld_avec, 32)
                dve.wait_ge(setT, NT)
                for k in range(KC):
                    if k:
                        dve.wait_ge(wa_made, 2 * H * k)
                    for h in range(H):
                        for j in range(2):
                            nc.vector.tensor_tensor_reduce(
                                out=q[:, h, cols(j, O)], in0=heads_w[:, k, h, :], in1=avec[h // 2][:, h % 2, cols(j, O)],
                                scale=1.0, scalar=0.0, op0=ALU.mult, op1=ALU.add,
                                accum_out=wa[:, k, j * H + h:j * H + h + 1]).then_inc(wa_made, 1)
                dve.wait_ge(wa_made, 2 * H * KC)
                lo_hT(0)
                link(nc.vector.tensor_copy(Wa[0][:, :, :], wa[:, :, :]))
                tt(Wa[1][:, :, :], wa[:, :, :], f32(Wa[0][:, :, :]), ALU.subtract).then_inc(wa_set, 1)
                for jt in range(NT):
                    dve.wait_ge(set_hi, 2 * KC + jt + 1)
                    tt(adjT[1][:, jt, :], ps[(OT + AC)[jt]][:, :], f32(adjT[0][:, jt, :]), ALU.subtract).then_inc(adj_set, 1)
                dve.wait_ge(ld_const, 16 * 6)
                dve.wait_ge(ids_made, 5)
                for k in range(2):
                    link(nc.vector.tensor_copy(bias[0:2, k, :], bias_f[k]))
                    link(tt(bias[32:34, k, :], bias_f[k], f32(bias[0:2, k, :]), ALU.subtract))
                feature_lo(0)
                feature_neg(0)
                masked(0, 0, 0)
                masked(0, 0, 1)
                values_lo(0, 0, 0)
                values_lo(0, 0, 1)
                leaky(0, 0, 0)
                leaky(0, 0, 1)
                masked(0, 1, 0)
                masked(0, 1, 1)
                inverse(0, 0)
                leaky(0, 1, 0)
                leaky(0, 1, 1)
                prob_lo(0, 0, 0)
                values_lo(0, 1, 0)
                values_lo(0, 1, 1)
                prob_lo(0, 0, 1)
                inverse(0, 1)
                elu(0, 0)
                prob_lo(0, 1, 0)
                values_lo(0, 2, 0)
                values_lo(0, 2, 1)
                prob_lo(0, 1, 1)

            def iteration(i, now):
                heads, ahead, behind = ("heads" in now), ("ahead" in now), ("behind" in now)
                b, c = i, i - 1
                if ahead:
                    statistics(0, xa, b + 1)
                if behind:
                    leaky(c, OUT, 0)
                    leaky(c, OUT, 1)
                if ahead:
                    shifts(0, b + 1)
                if heads:
                    masked(b, 2, 0)
                    masked(b, 2, 1)
                if behind:
                    inverse(c, OUT)
                if heads:
                    leaky(b, 2, 0)
                if ahead:
                    lo_hT(b + 1)
                if heads:
                    elu(b, 1)
                    values_lo(b, 3, 0)
                    values_lo(b, 3, 1)
                if behind:
                    prob_lo(c, OUT, 0)
                if heads:
                    leaky(b, 2, 1)
                if behind:
                    prob_lo(c, OUT, 1)
                if heads:
                    inverse(b, 2)
                    masked(b, 3, 0)
                if ahead:
                    feature_lo(b + 1)
                if heads:
                    masked(b, 3, 1)
                    leaky(b, 3, 0)
                    prob_lo(b, 2, 0)
                if behind:
                    elu(c, OUT)
                if heads:
                    prob_lo(b, 2, 1)
                if ahead:
                    feature_neg(b + 1)
                if heads:
                    leaky(b, 3, 1)
                if ahead:
                    masked(b + 1, 0, 0)
                if heads:
                    inverse(b, 3)
                if ahead:
                    masked(b + 1, 0, 1)
                if heads:
                    elu(b, 2)
                    prob_lo(b, 3, 0)
                if ahead:
                    leaky(b + 1, 0, 0)
                if heads:
                    prob_lo(b, 3, 1)
                if ahead:
                    leaky(b + 1, 0, 1)
                    masked(b + 1, 1, 0)
                    values_lo(b + 1, 0, 0)
                    masked(b + 1, 1, 1)
                    inverse(b + 1, 0)
                    leaky(b + 1, 1, 0)
                if heads:
                    elu(b, 3)
                if ahead:
                    leaky(b + 1, 1, 1)
                if behind:
                    ffn_statistics(c)
                    scale_y(c)
                if ahead:
                    values_lo(b + 1, 0, 1)
                if behind:
                    new_x(c)
                if ahead:
                    prob_lo(b + 1, 0, 0)
                    values_lo(b + 1, 1, 0)
                    inverse(b + 1, 1)
                    values_lo(b + 1, 1, 1)
                if heads:
                    out_values_lo(b)
                if ahead:
                    prob_lo(b + 1, 0, 1)
                if behind:
                    shifts(2, c)
                if heads:
                    out_scalars(b, 0)
                    out_scalars(b, 1)
                if ahead:
                    prob_lo(b + 1, 1, 0)
                    values_lo(b + 1, 2, 0)
                    prob_lo(b + 1, 1, 1)
                    values_lo(b + 1, 2, 1)
                if behind:
                    lo_h3T(c)
                if heads:
                    out_rows_lo(b)
                if behind:
                    message_lo(c, 0)
                    message_lo(c, 1)
                if ahead:
                    elu(b + 1, 0)
                if heads:
                    masked(b, OUT, 0)
                    masked(b, OUT, 1)
                if behind:
                    result(c, 0)
                    result(c, 1)

            program(dve, prologue, iteration)

        @block.gpsimd
        def _(pool):
            tt, ts = nc.gpsimd.tensor_tensor, nc.gpsimd.tensor_scalar

            def deviation(k, b):
                wait_apart(pool, ln_mv[k], b + 1)
                ts(ve[k][:, :], mv[k][:, :, 1], 1.0, EPS, ALU.mult, ALU.add).then_inc(ln_ve[k], 1)
                pool.wait_ge(ln_ve[k], b + 1)
                tt(rstd[k][:, :], ve[k][:, :], rsq[:, :], ALU.pow).then_inc(ln_rs[k], 1)

            def other_slope(b, u, half):
                n, was, p = unit(u, b), slot_before(u, b), pp[SLOT[u]]
                if half == 0 and was is not None:
                    pool.wait_ge(unit_transposed, NT * was + NT)
                pool.wait_ge(*((foneg_made, b + 1) if u == OUT else (f1neg_made, b + 1)))
                _, f1n = scalars(u)
                for t in (2 * half, 2 * half + 1):
                    wait_apart(pool, unit_masked, NT * n + t + 1)
                    ts(p[:, t, :], q[:, t, :], SLOPE, f1n[:, t:t + 1], ALU.mult, ALU.add).then_inc(unit_sloped, 1)

            def normalise_rows(b, u, half):
                n, p = unit(u, b), pp[SLOT[u]]
                wait_apart(pool, unit_inverse, n + 1)
                for t in (2 * half, 2 * half + 1):
                    ts(p[:, t, :], p[:, t, :], rinv[:, t:t + 1], 1.0, ALU.mult, ALU.mult).then_inc(unit_normalised, 1)

            def elu_lo(b, u):
                n, to = unit(u, b), outputs(u)
                for ot in range(KC):
                    pool.wait_ge(elu_hi_made, KC * n + ot + 1)
                    tt(to[1][:, ot, :], yb[:, ot, :], f32(to[0][:, ot, :]), ALU.subtract).then_inc(elu_lo_made, 1)

            def relu_lo(c):
                for dt in range(KC):
                    pool.wait_ge(relu_hi_made, KC * c + dt + 1)
                    tt(r[1][:, dt, :], relu_y[:, dt, :], f32(r[0][:, dt, :]), ALU.subtract).then_inc(relu_lo_made, 1)

            def add_beta(c):
                pool.wait_ge(residual_loaded, 16 * c + 16)
                for t in range(NT):
                    last = tt(xb[:, t, :], xb[:, t, :], beta[:, :], ALU.add)
                last.then_inc(beta_added, 1)

            def prologue():
                nc.gpsimd.memset(ident[:, :], 0.0).then_inc(ids_step, 1)
                nc.gpsimd.memset(pick_f, 0.0).then_inc(ids_step, 1)
                nc.gpsimd.memset(rsq[:, :], -0.5)
                pool.wait_ge(ids_step, 2)
                nc.gpsimd.affine_select(out=ident[:, :], in_=ident[:, :], compare_op=ALU.not_equal, fill=1.0, base=0,
                                        pattern=[[-1, P]], channel_multiplier=1).then_inc(ids_made, 1)
                for k, shift in enumerate((0, 32)):
                    nc.gpsimd.affine_select(out=pick_f[:, 0, :], in_=pick_f[:, 0, :], compare_op=ALU.not_equal, fill=1.0,
                                            base=-(1 + shift), pattern=[[0, P]], channel_multiplier=1)
                    nc.gpsimd.affine_select(out=pick_f[:, 1:5, :], in_=pick_f[:, 1:5, :], compare_op=ALU.not_equal, fill=1.0,
                                            base=-(H + shift), pattern=[[-1, H], [0, P]], channel_multiplier=1).then_inc(ids_step, 1)
                    pool.wait_ge(ids_step, 3 + k)
                wait_apart(pool, ids_made, 1)
                ts(ident_r[:, :], ident[:, :], 1.0, 1.0, ALU.mult, ALU.mult).then_inc(ids_made, 1)
                ts(pick[:, :, :], pick_f, 1.0, 1.0, ALU.mult, ALU.mult).then_inc(ids_made, 1)
                nc.gpsimd.memset(featrow[:, :].bitcast(F32), 0.0).then_inc(ids_made, 1)
                nc.gpsimd.memset(bias[:, :, :].bitcast(F32), 0.0)
                nc.gpsimd.memset(forow[:, :].bitcast(F32), 0.0).then_inc(ids_made, 1)
                pool.wait_ge(ids_made, 5)
                deviation(0, 0)
                for k in range(KC):
                    pool.wait_ge(set_hi, KC + k + 1)
                    tt(Wp[1][:, k, :], heads_w[:, k, :, :].rearrange("p h o -> p (h o)"), f32(Wp[0][:, k, :]), ALU.subtract)\
                        .then_inc(wp_set, 1)
                pool.wait_ge(ld_late, 16 * 3)
                late = ((Wo, wout_w), (F1, y[:, 0:KC, :]), (F2, y[:, KC:2 * KC, :]))
                for to, src in late:
                    ts(to[0][:, :, :], src, 1.0, 1.0, ALU.mult, ALU.mult).then_inc(late_hi, 1)
                for k, (to, src) in enumerate(late):
                    pool.wait_ge(late_hi, k + 1)
                    tt(to[1][:, :, :], src, f32(to[0][:, :, :]), ALU.subtract).then_inc(late_set, 1)
                other_slope(0, 0, 0)
                other_slope(0, 0, 1)
                other_slope(0, 1, 0)
                other_slope(0, 1, 1)
                normalise_rows(0, 0, 0)
                normalise_rows(0, 0, 1)
                normalise_rows(0, 1, 0)
                normalise_rows(0, 1, 1)
                elu_lo(0, 0)

            def iteration(i, now):
                heads, ahead, behind = ("heads" in now), ("ahead" in now), ("behind" in now)
                b, c = i, i - 1
                if ahead:
                    deviation(0, b + 1)
                if heads:
                    other_slope(b, 2, 0)
                if behind:
                    normalise_rows(c, OUT, 0)
                    normalise_rows(c, OUT, 1)
                if heads:
                    other_slope(b, 2, 1)
                    elu_lo(b, 1)
                    normalise_rows(b, 2, 0)
                    normalise_rows(b, 2, 1)
                    other_slope(b, 3, 0)
                    other_slope(b, 3, 1)
                if behind:
                    elu_lo(c, OUT)
                if heads:
                    normalise_rows(b, 3, 0)
                    normalise_rows(b, 3, 1)
                if ahead:
                    other_slope(b + 1, 0, 0)
                    other_slope(b + 1, 0, 1)
                if heads:
                    elu_lo(b, 2)
                if behind:
                    relu_lo(c)
                if ahead:
                    other_slope(b + 1, 1, 0)
                    other_slope(b + 1, 1, 1)
                if behind:
                    add_beta(c)
                if ahead:
                    normalise_rows(b + 1, 0, 0)
                    normalise_rows(b + 1, 0, 1)
                if behind:
                    deviation(1, c)
                if heads:
                    elu_lo(b, 3)
                if behind:
                    deviation(2, c)
                if ahead:
                    normalise_rows(b + 1, 1, 0)
                    normalise_rows(b + 1, 1, 1)
                    elu_lo(b + 1, 0)
                if heads:
                    other_slope(b, OUT, 0)
                    other_slope(b, OUT, 1)

            program(pool, prologue, iteration)


_INS = ["x", "adj", "L0_gnn_W_heads", "L0_gnn_a_heads", "L0_gnn_W_out", "L0_gnn_a_out", "L0_gnn_w1", "L0_gnn_b1",
        "L0_gnn_w2", "L0_gnn_b2", "L0_gnn_ln_gamma", "L0_gnn_ln_beta", "L1_gnn_W", "L1_gnn_b"]


def kernel(**inputs):
    import numpy as _np
    import concourse.bacc as _bacc
    from concourse import mybir as _mybir
    from concourse.bass_utils import run_bass_kernel_spmd as _run

    nc = _bacc.Bacc("TRN2", target_bir_lowering=False, num_devices=1)
    arrays, args = {}, []
    for name in _INS:
        a = _np.ascontiguousarray(inputs[name])
        arrays[f"in_{name}"] = a
        args.append(nc.dram_tensor(f"in_{name}", a.shape, _mybir.dt.from_np(a.dtype), kind="ExternalInput").ap())
    shape = arrays["in_x"].shape
    args.append(nc.dram_tensor("out_0", shape, _mybir.dt.float32, kind="ExternalOutput").ap())
    gnn_kernel(nc, *args)
    got = _run(nc, [arrays], core_ids=[0])
    return got.results[0]["out_0"]
```
